# Optimizing a Trainium2 kernel written in Bass

```python
import numpy as np
import jax
import jax.numpy as jnp

def _softmax(x, axis=-1):
    return jax.nn.softmax(x, axis=axis)

def _gelu(x):
    return jax.nn.gelu(x, approximate=True)

def _silu(x):
    return jax.nn.silu(x)

def _sigmoid(x):
    return jax.nn.sigmoid(x)

def _layernorm(x, axis=-1, eps=1e-05):
    m = jnp.mean(x, axis=axis, keepdims=True)
    v = jnp.var(x, axis=axis, keepdims=True)
    return (x - m) / jnp.sqrt(v + eps)

def _scatter_add(tgt, idx, src, axis=0):
    return tgt.at[idx].add(src)

def _segment_sum(src, seg, n):
    return jax.ops.segment_sum(src, seg, n)
kernel_name = 'mk_adaln_d1_jaxref_r2_b68617'

def setup_inputs(seed: int=0):
    np.random.seed(seed)
    _w = jnp.asarray

    def _L0_attn_setup():
        import jax, jax.numpy as jnp
        import numpy as np
        import math
        B, T, C = (64, 256, 512)
        LAYER_ID, N_LAYER = (6, 12)

        def _wkv(w, u, k, v):
            b, t, c = k.shape

            def step(carry, kv):
                aa, bb, pp = carry
                kt, vt = kv
                ww = u + kt
                q = jnp.maximum(pp, ww)
                e1 = jnp.exp(pp - q)
                e2 = jnp.exp(ww - q)
                y = (e1 * aa + e2 * vt) / (e1 * bb + e2)
                ww2 = pp + w
                q2 = jnp.maximum(ww2, kt)
                e1 = jnp.exp(ww2 - q2)
                e2 = jnp.exp(kt - q2)
                return ((e1 * aa + e2 * vt, e1 * bb + e2, q2), y)
            init = (jnp.zeros((b, c), k.dtype), jnp.zeros((b, c), k.dtype), jnp.full((b, c), -1e+38, k.dtype))
            _, ys = jax.lax.scan(step, init, (jnp.swapaxes(k, 0, 1), jnp.swapaxes(v, 0, 1)))
            return jnp.swapaxes(ys, 0, 1)
        key = jax.random.key(seed)
        k1, k2, k3, k4, k5 = jax.random.split(key, 5)
        r01 = LAYER_ID / N_LAYER
        r10 = 1.0 - r01
        i = jnp.arange(C, dtype=jnp.float32)
        ddd = i / C
        time_decay = -5.0 + 8.0 * (i / (C - 1)) ** (0.7 + 1.3 * r01)
        zigzag = ((jnp.arange(C) + 1) % 3 - 1).astype(jnp.float32) * 0.5
        time_first = jnp.full((C,), math.log(0.3), jnp.float32) + zigzag
        time_mix_k = (ddd ** r10).reshape(1, 1, C)
        time_mix_v = (ddd ** r10 + 0.3 * r01).reshape(1, 1, C)
        time_mix_r = (ddd ** (0.5 * r10)).reshape(1, 1, C)
        x = jax.random.normal(k1, (B, T, C), jnp.float32)
        Wk = jax.random.normal(k2, (C, C), jnp.float32) * 0.02
        Wv = jax.random.normal(k3, (C, C), jnp.float32) * 0.02
        Wr = jax.random.normal(k4, (C, C), jnp.float32) * 0.02
        Wo = jax.random.normal(k5, (C, C), jnp.float32) * 0.02
        return {'x': x, 'time_decay': time_decay, 'time_first': time_first, 'time_mix_k': time_mix_k, 'time_mix_v': time_mix_v, 'time_mix_r': time_mix_r, 'Wk': Wk, 'Wv': Wv, 'Wr': Wr, 'Wo': Wo}
    _L0_attn_in = _L0_attn_setup()

    def _L0_ffn_setup():
        import jax, jax.numpy as jnp
        import numpy as np
        NUM_EXPERTS = 8
        TOP_K = 2
        HIDDEN = 512
        INTER_TOTAL = 4096
        B, S = (2, 1024)
        key = jax.random.key(seed)
        k1, k2, k3, k4, k5, k6 = jax.random.split(key, 6)
        T = B * S
        x = jax.random.normal(k1, (B, S, HIDDEN), dtype=jnp.float32)
        scores = jax.random.uniform(k2, (T, NUM_EXPERTS), dtype=jnp.float32)
        expert_weights = jax.random.uniform(k3, (T, TOP_K), dtype=jnp.float32)
        top_experts = jax.random.randint(k4, (T, TOP_K), 0, NUM_EXPERTS, dtype=jnp.int32)
        w1 = jax.random.normal(k5, (HIDDEN, INTER_TOTAL), dtype=jnp.float32) * 0.02
        w2 = jax.random.normal(k6, (INTER_TOTAL, HIDDEN), dtype=jnp.float32) * 0.02
        return {'x': x, 'scores': scores, 'expert_weights': expert_weights, 'top_experts': top_experts, 'w1': w1, 'w2': w2}
    _L0_ffn_in = _L0_ffn_setup()
    _L0_c = _w((lambda *s: np.random.randn(*s).astype(np.float32) * 0.05)(8, 512))
    _L0_wmod = _w((lambda *s: np.random.randn(*s).astype(np.float32) * 0.05)(512, 6 * 512) * 512 ** (-0.5))
    _d = {'L0_attn_x': _L0_attn_in['x'], 'L0_attn_time_decay': _L0_attn_in['time_decay'], 'L0_attn_time_first': _L0_attn_in['time_first'], 'L0_attn_time_mix_k': _L0_attn_in['time_mix_k'], 'L0_attn_time_mix_v': _L0_attn_in['time_mix_v'], 'L0_attn_time_mix_r': _L0_attn_in['time_mix_r'], 'L0_attn_Wk': _L0_attn_in['Wk'], 'L0_attn_Wv': _L0_attn_in['Wv'], 'L0_attn_Wr': _L0_attn_in['Wr'], 'L0_attn_Wo': _L0_attn_in['Wo'], 'L0_ffn_scores': _L0_ffn_in['scores'], 'L0_ffn_expert_weights': _L0_ffn_in['expert_weights'], 'L0_ffn_top_experts': _L0_ffn_in['top_experts'], 'L0_ffn_w1': _L0_ffn_in['w1'], 'L0_ffn_w2': _L0_ffn_in['w2'], 'L0_c': _L0_c, 'L0_wmod': _L0_wmod}
    _x0 = _d['L0_attn_x']
    _d['L0_attn_x'] = jax.random.normal(jax.random.fold_in(jax.random.key(seed), 1), (8, 1024, 512), dtype=_x0.dtype)
    del _x0
    return _d

def reference(L0_attn_x, L0_attn_time_decay, L0_attn_time_first, L0_attn_time_mix_k, L0_attn_time_mix_v, L0_attn_time_mix_r, L0_attn_Wk, L0_attn_Wv, L0_attn_Wr, L0_attn_Wo, L0_ffn_scores, L0_ffn_expert_weights, L0_ffn_top_experts, L0_ffn_w1, L0_ffn_w2, L0_c, L0_wmod):

    def _L0_attn_ref(x, time_decay, time_first, time_mix_k, time_mix_v, time_mix_r, Wk, Wv, Wr, Wo):
        import jax, jax.numpy as jnp
        import numpy as np
        import math
        B, T, C = (64, 256, 512)
        LAYER_ID, N_LAYER = (6, 12)

        def _wkv(w, u, k, v):
            b, t, c = k.shape

            def step(carry, kv):
                aa, bb, pp = carry
                kt, vt = kv
                ww = u + kt
                q = jnp.maximum(pp, ww)
                e1 = jnp.exp(pp - q)
                e2 = jnp.exp(ww - q)
                y = (e1 * aa + e2 * vt) / (e1 * bb + e2)
                ww2 = pp + w
                q2 = jnp.maximum(ww2, kt)
                e1 = jnp.exp(ww2 - q2)
                e2 = jnp.exp(kt - q2)
                return ((e1 * aa + e2 * vt, e1 * bb + e2, q2), y)
            init = (jnp.zeros((b, c), k.dtype), jnp.zeros((b, c), k.dtype), jnp.full((b, c), -1e+38, k.dtype))
            _, ys = jax.lax.scan(step, init, (jnp.swapaxes(k, 0, 1), jnp.swapaxes(v, 0, 1)))
            return jnp.swapaxes(ys, 0, 1)
        xx = jnp.pad(x, ((0, 0), (1, 0), (0, 0)))[:, :-1]
        xk = x * time_mix_k + xx * (1.0 - time_mix_k)
        xv = x * time_mix_v + xx * (1.0 - time_mix_v)
        xr = x * time_mix_r + xx * (1.0 - time_mix_r)
        k = jnp.einsum('btc,dc->btd', xk, Wk)
        v = jnp.einsum('btc,dc->btd', xv, Wv)
        sr = jax.nn.sigmoid(jnp.einsum('btc,dc->btd', xr, Wr))
        w = -jnp.exp(time_decay)
        rwkv = sr * _wkv(w, time_first, k, v)
        return jnp.einsum('btc,dc->btd', rwkv, Wo)

    def _L0_ffn_ref(x, scores, expert_weights, top_experts, w1, w2):
        import jax, jax.numpy as jnp
        import numpy as np
        NUM_EXPERTS = 8
        TOP_K = 2
        HIDDEN = 512
        INTER_TOTAL = 4096
        B, S = (2, 1024)
        in_shape = x.shape
        T = in_shape[0] * in_shape[1]
        H = in_shape[-1]
        x_flat = x.reshape(T, H)
        flat_experts = top_experts.reshape(-1)
        flat_weights = expert_weights.reshape(-1)
        order = jnp.argsort(flat_experts, stable=True)
        token_idx = order // TOP_K
        xg = x_flat[token_idx]
        h = jax.nn.gelu(xg @ w1, approximate=True)
        y = h @ w2
        w_sorted = flat_weights[order]
        out = jnp.zeros((T, H), dtype=x.dtype).at[token_idx].add(w_sorted[:, None] * y)
        return out.reshape(in_shape)
    x = L0_attn_x
    mod = (_silu(L0_c) @ L0_wmod).reshape(L0_c.shape[0], 6, 1, -1)
    sa, ca, ga, sb, cb, gb = (mod[:, 0], mod[:, 1], mod[:, 2], mod[:, 3], mod[:, 4], mod[:, 5])
    ga = (2 * (ga >= 0) - 1) * jnp.maximum(jnp.abs(ga), 0.25)
    gb = (2 * (gb >= 0) - 1) * jnp.maximum(jnp.abs(gb), 0.25)
    h = _layernorm(x, axis=-1) * (1 + ca) + sa
    x = x + ga * _L0_attn_ref(h, L0_attn_time_decay, L0_attn_time_first, L0_attn_time_mix_k, L0_attn_time_mix_v, L0_attn_time_mix_r, L0_attn_Wk, L0_attn_Wv, L0_attn_Wr, L0_attn_Wo)
    h = _layernorm(x, axis=-1) * (1 + cb) + sb
    x = x + gb * _L0_ffn_ref(h, L0_ffn_scores, L0_ffn_expert_weights, L0_ffn_top_experts, L0_ffn_w1, L0_ffn_w2)
    return x

_drawn_inputs = setup_inputs


def setup_inputs(seed=0):
    import zlib

    import numpy as np

    out = dict(_drawn_inputs(seed))
    spreads = {}
    factors = {'L0_attn_time_decay': 5.72,
     'L0_attn_time_first': 28.459,
     'L0_attn_time_mix_k': 8.0,
     'L0_attn_time_mix_v': 8.0,
     'L0_attn_time_mix_r': 8.0,
     'L0_attn_Wk': 8.0,
     'L0_attn_Wv': 4.811,
     'L0_attn_Wr': 8.0,
     'L0_attn_Wo': 4.817,
     'L0_ffn_expert_weights': 23.709,
     'L0_ffn_w1': 2.879,
     'L0_ffn_w2': 2.733}
    for name, (base, spread) in spreads.items():
        noise = np.random.default_rng([zlib.crc32(name.encode()), seed]).standard_normal(out[name].shape)
        drawn = base * np.exp(spread * noise) if base else spread * noise
        out[name] = jnp.asarray(drawn.astype(out[name].dtype))
    for name, factor in factors.items():
        out[name] = (out[name] * factor).astype(out[name].dtype)
    return out
```

```python
from contextlib import ExitStack

import concourse.bass as bass
from concourse import mybir

P = 128
F32 = mybir.dt.float32
F32R = mybir.dt.float32r
ALU = mybir.AluOpType
ACT = mybir.ActivationFunctionType

EPS = 1e-5
LN_EXP_SET = 6
NEG_HUGE = -1e38
GATE_FLOOR = 0.25

B, T, C = 8, 1024, 512
CT = C // P
ST = 512
TT_ = ST // P
STEPS = B * T // ST
NTOK = 2048
FT = 4
FH = 4096
GROUPS = FH // (FT * P)
CHUNKS = NTOK // ST
TOKT = NTOK // P
MK, MV, MR, MO = range(4)
SCALE1, SHIFT1, SCALE2, SHIFT2 = range(4)


def attention(nc, io, per, scratch, out):
    with ExitStack() as ctx:
        def sb(name, shape, dt=F32):
            return ctx.enter_context(nc.sbuf_tensor(name, shape, dt))

        def sem(name):
            return ctx.enter_context(nc.semaphore(name))

        xin = sb("xin", [P, 2, TT_, C])
        xres = sb("xres", [P, TT_, C])
        gate = sb("gate", [P, C])
        bn6 = sb("bn6", [P, TT_, 6])
        mv = sb("mv", [P, TT_, 2])
        lnv = sb("lnv", [P, TT_])
        rstd = sb("rstd", [P, TT_])
        nmr = sb("nmr", [P, TT_])
        mod = sb("mod", [P, 2, CT])
        hT = sb("hT", [P, CT, ST + 1])
        mix = sb("mix", [P, 2, 3, CT, ST])
        state = sb("state", [P, 2, 3, 2, ST + 1])
        kb = sb("kb", [P, 2, 2, ST])
        vb = sb("vb", [P, 2, 2, ST])
        mb = sb("mb", [P, 2, 2, ST])
        eb = sb("eb", [P, 2, 2, ST])
        kp = sb("kp", [P, 2, ST])
        ha = sb("ha", [P, 2, ST])
        e1 = sb("e1", [P, 2, ST])
        ga = sb("ga", [P, 2, ST])
        gb = sb("gb", [P, 2, ST])
        yT = sb("yT", [P, 2, CT, ST])
        proj = [ctx.enter_context(nc.psum_tensor(f"proj{m}", [P, 2, ST], F32)) for m in range(3)]
        misc = ctx.enter_context(nc.psum_tensor("misc", [P, 2, ST], F32))

        c_in = gate[0:B, :]
        chan_rows = e1[0:5 * CT, 0, 0:P]
        w_raw = [t[:].rearrange("p a b c -> p (a b) c") for t in (kb, vb, mb, eb)]
        spare = mix[:, 1].rearrange("p m c t -> p (m c t)")
        wmod1 = spare[:, 0:2 * CT * C].rearrange("p (k n) -> p k n", k=CT)
        wmod_ga = spare[:, 2 * CT * C:3 * CT * C].rearrange("p (k n) -> p k n", k=CT)
        wmod2 = yT[:].rearrange("p h c t -> p (h c t)").rearrange("p (k n) -> p k n", k=CT)
        wmod_gb = xres
        gate_rows = xres[0:B, 0:2, :]
        siluT = sb("siluT", [P, CT, B])
        silu_exp = sb("silu_exp", [P, CT, B])
        silu_den = sb("silu_den", [P, CT, B])
        silu_rec = sb("silu_rec", [P, CT, B])
        g_work = sb("g_work", [P, 6, 2, CT, B])
        chan_ps = misc[:, 0, 0:5 * CT]
        cT_ps = misc[:, 1, 0:CT * B].rearrange("p (k b) -> p k b", k=CT)
        mod1_ps = proj[1][:, 1, 0:2 * CT * B].rearrange("p (q c b) -> p q c b", q=2, c=CT)
        mod2_ps = misc[:, 0, 0:2 * CT * B].rearrange("p (q c b) -> p q c b", q=2, c=CT)
        gT_ps = misc[:, 0, 64:64 + 2 * CT * B].rearrange("p (g c b) -> p g c b", g=2, c=CT)

        c_loaded = sem("c_loaded")
        chan_loaded = sem("chan_loaded")
        w_loaded = [sem(f"w_loaded{m}") for m in range(4)]
        wmod1_loaded = sem("wmod1_loaded")
        wmod_ga_loaded = sem("wmod_ga_loaded")
        wmod2_loaded = sem("wmod2_loaded")
        wmod_gb_loaded = sem("wmod_gb_loaded")
        ident_zero = sem("ident_zero")
        ident_ready = sem("ident_ready")
        eps_ready = sem("eps_ready")
        chan_in_psum = sem("chan_in_psum")
        chan_ready = sem("chan_ready")
        const_ready = sem("const_ready")
        decay_ready = sem("decay_ready")
        cT_in_psum = sem("cT_in_psum")
        c_exp_ready = sem("c_exp_ready")
        silu_step = sem("silu_step")
        mod1_in_psum = sem("mod1_in_psum")
        mod1_ready = sem("mod1_ready")
        mod2_in_psum = sem("mod2_in_psum")
        g_floor = sem("g_floor")
        g_step = sem("g_step")
        mod2_ready = sem("mod2_ready")
        gate_rows_in_psum = sem("gate_rows_in_psum")
        gate_rows_ready = sem("gate_rows_ready")
        gates_stored = sem("gates_stored")
        wt_in_psum = sem("wt_in_psum")
        wt_even = sem("wt_even")
        wt_odd = sem("wt_odd")

        x_loaded = [sem("x_loaded0"), sem("x_loaded1")]
        xres_loaded = sem("xres_loaded")
        gate_loaded = sem("gate_loaded")
        out_stored = sem("out_stored")
        mod_ready = sem("mod_ready")
        bn_ready = sem("bn_ready")
        mv_ready = sem("mv_ready")
        lnv_ready = sem("lnv_ready")
        rstd_ready = sem("rstd_ready")
        nmr_ready = sem("nmr_ready")
        xn_ready = sem("xn_ready")
        xnT_in_psum = sem("xnT_in_psum")
        shift_ready = sem("shift_ready")
        hT_ready = sem("hT_ready")
        mixprod_ready = sem("mixprod_ready")
        mix_ready = sem("mix_ready")
        in_psum = [sem("k_in_psum"), sem("v_in_psum"), sem("r_in_psum")]
        k_ready = sem("k_ready")
        v_ready = sem("v_ready")
        m_ready = sem("m_ready")
        absr_ready = sem("absr_ready")
        eb_ready = sem("eb_ready")
        init_ready = sem("init_ready")
        max_ready = sem("max_ready")
        kp_ready = sem("kp_ready")
        e1_arg = sem("e1_arg")
        ha_arg = sem("ha_arg")
        ga_arg = sem("ga_arg")
        gb_arg = sem("gb_arg")
        e1_ready = sem("e1_ready")
        ha_ready = sem("ha_ready")
        ga_ready = sem("ga_ready")
        gb_ready = sem("gb_ready")
        den_state = sem("den_state")
        e2v_ready = sem("e2v_ready")
        num_state = sem("num_state")
        n2_ready = sem("n2_ready")
        n1_ready = sem("n1_ready")
        d1_ready = sem("d1_ready")
        den_ready = sem("den_ready")
        full_den_ready = sem("full_den_ready")
        log_ready = sem("log_ready")
        logm_ready = sem("logm_ready")
        inv_ready = sem("inv_ready")
        num_ready = sem("num_ready")
        y_ready = sem("y_ready")
        o_in_psum = sem("o_in_psum")
        gated_ready = sem("gated_ready")
        res_ready = sem("res_ready")

        x_rows = io["x"].rearrange("(s t p) c -> s p t c", t=TT_, p=P)
        out_rows = out.rearrange("(s t p) c -> s p t c", t=TT_, p=P)
        block = ctx.enter_context(nc.Block())

        def over_batches(eng, batch):
            batch(0, first=True, last=False)
            with eng.Fori(1, B - 1) as b:
                batch(b, first=False, last=False)
            batch(B - 1, first=False, last=True)

        @block.sync
        def _(sp):
            def load_x(b, h):
                s = b * 2 + h
                sp.dma_start(xin[:, h], x_rows[bass.ds(s, 1)].rearrange("o p t c -> (o p) t c")
                             ).then_inc(x_loaded[h], 16)

            def residual(b, h, step, wait_stored):
                if wait_stored:
                    sp.wait_ge(out_stored, step * 16)
                sp.dma_start(xres[:], x_rows[bass.ds(step, 1)].rearrange("o p t c -> (o p) t c")
                             ).then_inc(xres_loaded, 16)
                if h == 0:
                    if wait_stored:
                        sp.wait_ge(gated_ready, step * 4)
                    sp.dma_start(gate[:], scratch["gates"][0, bass.ds(b, 1), :].to_broadcast([P, C])
                                 ).then_inc(gate_loaded, 16)
                sp.wait_ge(res_ready, step * 4 + 4)
                sp.dma_start(out_rows[bass.ds(step, 1)].rearrange("o p t c -> (o p) t c"), xres[:]
                             ).then_inc(out_stored, 16)

            sp.dma_start(c_in, io["c"]).then_inc(c_loaded, 16)
            for i, name in enumerate(("mix_k", "mix_v", "mix_r", "decay", "first")):
                sp.dma_start(chan_rows[i * CT:(i + 1) * CT, :], io[name].rearrange("(c p) -> c p", p=P)
                             ).then_inc(chan_loaded, 16)
            load_x(0, 0)
            wmod_rows = io["wmod"].rearrange("(k p) n -> p k n", p=P)
            sp.dma_start(wmod1, wmod_rows[:, :, 0:2 * C]).then_inc(wmod1_loaded, 16)
            for m, name in enumerate(("Wk", "Wv", "Wr", "Wo")):
                sp.dma_start(w_raw[m], io[name].rearrange("(t p) c -> p t c", p=P)).then_inc(w_loaded[m], 16)
            load_x(0, 1)
            sp.dma_start(wmod_ga, wmod_rows[:, :, 2 * C:3 * C]).then_inc(wmod_ga_loaded, 16)
            sp.dma_start(wmod2, wmod_rows[:, :, 3 * C:5 * C]).then_inc(wmod2_loaded, 16)
            sp.dma_start(wmod_gb[:], wmod_rows[:, :, 5 * C:6 * C]).then_inc(wmod_gb_loaded, 16)
            sp.wait_ge(gate_rows_ready, 2)
            sp.dma_start(scratch["gates"].rearrange("g b c -> b g c"), gate_rows).then_inc(gates_stored, 16)
            sp.wait_ge(gates_stored, 16)

            def batch(b, first, last):
                for h in range(2):
                    s = b * 2 + h
                    if not last:
                        sp.wait_ge(xnT_in_psum, s * 4 + 4)
                        load_x(b + 1, h)
                    if not (first and h == 0):
                        if h == 0:
                            residual(b - 1, 1, s - 1, True)
                        else:
                            residual(b, 0, s - 1, not first)
            over_batches(sp, batch)
            residual(B - 1, 1, STEPS - 1, True)
            sp.wait_ge(out_stored, STEPS * 16)

        @block.gpsimd
        def _(pool):
            pool.memset(per["ident"][:], 0.0).then_inc(ident_zero, 1)
            pool.memset(per["eps"][:], EPS).then_inc(eps_ready, 1)
            pool.wait_ge(ident_zero, 1)
            pool.affine_select(out=per["ident"][:], in_=per["ident"][:], compare_op=ALU.not_equal, fill=1.0, base=0,
                               pattern=[[-1, P]], channel_multiplier=1).then_inc(ident_ready, 1)

        @block.scalar
        def _(act):
            def transposed_weights(m):
                for c in range(0, CT, 2):
                    act.wait_ge(wt_in_psum, 4 * m + c + 1)
                    nc.scalar.activation(per["wT"][:, m, c, :], proj[2][:, 0], ACT.Copy).then_inc(wt_even, 1)

            def rstd_of(s):
                act.wait_ge(mv_ready, s * 4 + 4)
                nc.scalar.activation(lnv[:], mv[:, :, 1], ACT.Ln, bias=per["eps"][:, 0:1]).then_inc(lnv_ready, 1)
                act.wait_ge(lnv_ready, s + 1)
                nc.scalar.activation(rstd[:], lnv[:], ACT.Exp, scale=-0.5).then_inc(rstd_ready, 1)

            def normalise(s, h):
                act.wait_ge(nmr_ready, s + 1)
                for t in range(TT_):
                    nc.scalar.activation(xin[:, h, t], xin[:, h, t], ACT.Identity, bias=nmr[:, t:t + 1],
                                         scale=rstd[:, t:t + 1]).then_inc(xn_ready, 1)

            def modulate(s, h, b, first_step):
                act.wait_ge(mod_ready, b + 1)
                act.wait_ge(shift_ready, s + 1)
                if not first_step:
                    act.wait_ge(mix_ready, s * 12)
                for c in range(CT):
                    act.wait_ge(xnT_in_psum, s * 4 + c + 1)
                    nc.scalar.activation(hT[:, c, 1:ST + 1], misc[:, c % 2], ACT.Identity,
                                         bias=mod[:, SHIFT1, c:c + 1], scale=mod[:, SCALE1, c:c + 1]
                                         ).then_inc(hT_ready, 1)

            def mixprods(s, h, m, wait_free):
                if wait_free:
                    act.wait_ge(in_psum[m], s * 2 - 2)
                for c in range(CT):
                    if m == 0:
                        act.wait_ge(hT_ready, s * 4 + c + 1)
                    nc.scalar.activation(mix[:, h, m, c], hT[:, c, 1:ST + 1], ACT.Copy,
                                         scale=per["chan"][:, m, c:c + 1]).then_inc(mixprod_ready, 1)

            def evacuate_kv(u, q, m, old):
                act.wait_ge(in_psum[m], u + 1)
                if old:
                    if m == 0:
                        act.wait_ge(kp_ready, u - 1)
                    else:
                        act.wait_ge(n2_ready, u - 1)
                nc.scalar.activation((kb if m == 0 else vb)[:, q], proj[m][:], ACT.Copy
                                     ).then_inc(k_ready if m == 0 else v_ready, 1)

            def evacuate_r(u, q, old):
                act.wait_ge(in_psum[2], u + 1)
                if old:
                    act.wait_ge(logm_ready, u - 1)
                nc.scalar.activation(mb[:, q], proj[2][:], ACT.Relu, scale=-1.0).then_inc(m_ready, 1)
                nc.scalar.activation(eb[:, q], proj[2][:], ACT.Abs).then_inc(absr_ready, 1)
                act.wait_ge(absr_ready, u + 1)
                nc.scalar.activation(eb[:, q], eb[:, q], ACT.Exp, scale=-1.0).then_inc(eb_ready, 1)

            def state_weights(u, p):
                act.wait_ge(kp_ready, u + 1)
                for i in range(2):
                    c = 2 * p + i
                    nc.scalar.activation(e1[:, i], kp[:, i], ACT.Relu, bias=per["neg_w"][:, c:c + 1]
                                         ).then_inc(e1_arg, 1)
                    nc.scalar.activation(ha[:, i], kp[:, i], ACT.Relu, bias=per["w"][:, c:c + 1], scale=-1.0
                                         ).then_inc(ha_arg, 1)
                act.wait_ge(e1_arg, u * 2 + 2)
                nc.scalar.activation(e1[:], e1[:], ACT.Exp, scale=-1.0).then_inc(e1_ready, 1)
                act.wait_ge(ha_arg, u * 2 + 2)
                nc.scalar.activation(ha[:], ha[:], ACT.Exp, scale=-1.0).then_inc(ha_ready, 1)

            def output_weights(u, p):
                for i in range(2):
                    c = 2 * p + i
                    nc.scalar.activation(ga[:, i], kp[:, i], ACT.Relu, bias=per["neg_u"][:, c:c + 1], scale=-1.0
                                         ).then_inc(ga_arg, 1)
                    nc.scalar.activation(gb[:, i], kp[:, i], ACT.Relu, bias=per["chan"][:, 4, c:c + 1]
                                         ).then_inc(gb_arg, 1)
                act.wait_ge(ga_arg, u * 2 + 2)
                nc.scalar.activation(ga[:], ga[:], ACT.Exp, scale=-1.0).then_inc(ga_ready, 1)
                act.wait_ge(gb_arg, u * 2 + 2)
                nc.scalar.activation(gb[:], gb[:], ACT.Exp, scale=-1.0).then_inc(gb_ready, 1)

            def log_den(u):
                act.wait_ge(full_den_ready, u + 1)
                nc.scalar.activation(ga[:], ga[:], ACT.Ln).then_inc(log_ready, 1)

            def inverse(u):
                act.wait_ge(logm_ready, u + 1)
                nc.scalar.activation(ga[:], ga[:], ACT.Exp, scale=-1.0).then_inc(inv_ready, 1)

            act.add_instruction(mybir.InstLoadActFuncSet(name=nc.get_next_instruction_name(),
                                                         act_func_set_id=LN_EXP_SET, ins=[], outs=[]))
            act.wait_ge(cT_in_psum, 1)
            nc.scalar.activation(silu_exp[:], cT_ps, ACT.Exp, scale=-1.0).then_inc(c_exp_ready, 1)
            act.wait_ge(chan_ready, 1)
            nc.scalar.activation(per["neg_w"][:], per["chan"][:, 3, :], ACT.Exp).then_inc(decay_ready, 1)
            act.wait_ge(eps_ready, 1)
            rstd_of(0)
            normalise(0, 0)
            modulate(0, 0, 0, True)
            mixprods(0, 0, 0, False)
            transposed_weights(0)
            transposed_weights(1)
            mixprods(0, 0, 1, False)
            transposed_weights(2)
            mixprods(0, 0, 2, False)
            transposed_weights(3)
            evacuate_kv(0, 0, 0, False)
            rstd_of(1)
            normalise(1, 1)

            def batch(b, first, last):
                for h in range(2):
                    s = b * 2 + h
                    u = b * 4 + 2 * h
                    ahead = not (last and h == 1)
                    nb = b + h
                    behind = not (first and h == 0)
                    state_weights(u, 0)
                    evacuate_kv(u, 0, 1, behind)
                    output_weights(u, 0)
                    evacuate_r(u, 0, behind)
                    if not last:
                        rstd_of(s + 2)
                    if ahead:
                        modulate(s + 1, 1 - h, nb, False)
                        if not behind:
                            act.wait_ge(mod2_in_psum, 1)
                        mixprods(s + 1, 1 - h, 0, behind)
                    log_den(u)
                    if ahead:
                        mixprods(s + 1, 1 - h, 1, behind)
                    inverse(u)
                    if ahead:
                        mixprods(s + 1, 1 - h, 2, behind)
                    evacuate_kv(u + 1, 1, 0, behind)
                    state_weights(u + 1, 1)
                    evacuate_kv(u + 1, 1, 1, behind)
                    output_weights(u + 1, 1)
                    evacuate_r(u + 1, 1, behind)
                    if not last:
                        normalise(s + 2, h)
                    log_den(u + 1)
                    inverse(u + 1)
                    if ahead:
                        evacuate_kv(u + 2, 0, 0, True)
            over_batches(act, batch)

        @block.tensor
        def _(pe):
            def transposes(s, h, cs, old):
                pe.wait_ge(xn_ready, s * 4 + 4)
                for c in cs:
                    if c >= 2:
                        pe.wait_ge(hT_ready, s * 4 + c - 1)
                    elif old:
                        pe.wait_ge(res_ready, s * 4 - 9 + c)
                    for t in range(TT_):
                        last = nc.tensor.transpose(misc[:, c % 2, t * P:(t + 1) * P], xin[:, h, t, c * P:(c + 1) * P],
                                                   per["ident"][:])
                    last.then_inc(xnT_in_psum, 1)

            def project(s, h, p, u, ms, old):
                for m in ms:
                    pe.wait_ge(mix_ready, s * 12 + 4 * m + 4)
                    if old:
                        pe.wait_ge((k_ready, v_ready, absr_ready)[m], u)
                    for i in range(2):
                        d = 2 * p + i
                        for c in range(CT):
                            last = nc.tensor.matmul(proj[m][:, i], per["wT"][:, m, c, d * P:(d + 1) * P],
                                                    mix[:, h, m, c], start=(c == 0), stop=(c == CT - 1))
                    last.then_inc(in_psum[m], 1)

            def out_project(s, h, ts, ahead):
                pe.wait_ge(y_ready, s * 2 + 2)
                for t in ts:
                    if t >= 2:
                        pe.wait_ge(res_ready, s * 4 + t - 1)
                    elif ahead:
                        pe.wait_ge(hT_ready, s * 4 + 8 + t + 3)
                    else:
                        pe.wait_ge(res_ready, s * 4 - 1 + t)
                    for c in range(CT):
                        last = nc.tensor.matmul(misc[:, t % 2], yT[:, h, c, t * P:(t + 1) * P], per["wT"][:, MO, c, :],
                                                start=(c == 0), stop=(c == CT - 1))
                    last.then_inc(o_in_psum, 1)

            def transpose_weights(m):
                pe.wait_ge(w_loaded[m], 16)
                for c in range(CT):
                    if m or c >= 2:
                        pe.wait_ge((wt_even, wt_odd)[c % 2], 2 * m + c // 2)
                    for t in range(CT):
                        last = nc.tensor.transpose(proj[2][:, c % 2, t * P:(t + 1) * P],
                                                   w_raw[m][:, t, c * P:(c + 1) * P], per["ident"][:])
                    last.then_inc(wt_in_psum, 1)

            def modulation(dest, w, col):
                for c in range(CT):
                    for k in range(CT):
                        last = nc.tensor.matmul(dest[:, c, :], w[:, k, col * C + c * P:col * C + (c + 1) * P],
                                                siluT[:, k, :], start=(k == 0), stop=(k == CT - 1))
                return last

            pe.wait_ge(ident_ready, 1)
            pe.wait_ge(chan_loaded, 80)
            nc.tensor.transpose(chan_ps, chan_rows, per["ident"][0:5 * CT, 0:5 * CT]).then_inc(chan_in_psum, 1)
            pe.wait_ge(c_loaded, 16)
            for k in range(CT):
                last = nc.tensor.transpose(cT_ps[:, k, :], c_in[:, k * P:(k + 1) * P], per["ident"][0:B, 0:B])
            last.then_inc(cT_in_psum, 1)
            pe.wait_ge(silu_step, 3)
            pe.wait_ge(wmod1_loaded, 16)
            modulation(mod1_ps[:, SCALE1], wmod1, 1)
            modulation(mod1_ps[:, SHIFT1], wmod1, 0).then_inc(mod1_in_psum, 1)
            pe.wait_ge(chan_ready, 1)
            transposes(0, 0, range(CT), False)
            transpose_weights(MK)
            transpose_weights(MV)
            pe.wait_ge(wt_even, 2)
            pe.wait_ge(wt_odd, 2)
            project(0, 0, 0, 0, range(0, 1), False)
            transpose_weights(MR)
            pe.wait_ge(mod1_ready, 2)
            project(0, 0, 0, 0, range(1, 2), False)
            transpose_weights(MO)
            pe.wait_ge(wt_even, 8)
            pe.wait_ge(wt_odd, 8)
            project(0, 0, 0, 0, range(2, 3), False)
            pe.wait_ge(hT_ready, 4)
            pe.wait_ge(wmod_ga_loaded, 16)
            modulation(gT_ps[:, 0], wmod_ga, 0)
            pe.wait_ge(wmod2_loaded, 16)
            modulation(mod2_ps[:, SCALE2 - 2], wmod2, 1)
            modulation(mod2_ps[:, SHIFT2 - 2], wmod2, 0)
            pe.wait_ge(wmod_gb_loaded, 16)
            modulation(gT_ps[:, 1], wmod_gb, 0).then_inc(mod2_in_psum, 1)
            pe.wait_ge(g_step, 5)
            pe.wait_ge(mod2_ready, 2)
            for g in range(2):
                for c in range(CT):
                    last = nc.tensor.transpose(misc[0:B, 1 - g, c * P:(c + 1) * P], g_work[:, 5, g, c, :],
                                               per["ident"][:])
            last.then_inc(gate_rows_in_psum, 1)
            pe.wait_ge(gate_rows_ready, 2)

            def batch(b, first, last):
                for h in range(2):
                    s = b * 2 + h
                    u = b * 4 + 2 * h
                    ahead = not (last and h == 1)
                    if ahead:
                        if first:
                            pe.wait_ge(hT_ready, s * 4 + 4)
                        transposes(s + 1, 1 - h, range(0, 2), not first)
                    project(s, h, 1, u + 1, range(0, 2), True)
                    if ahead:
                        transposes(s + 1, 1 - h, range(2, 4), not first)
                    project(s, h, 1, u + 1, range(2, 3), True)
                    behind = not (first and h == 0)
                    if behind:
                        out_project(s - 1, 1 - h, range(0, 2), ahead)
                    if ahead:
                        project(s + 1, 1 - h, 0, u + 2, range(0, 1), True)
                    if behind:
                        out_project(s - 1, 1 - h, range(2, 4), ahead)
                    if ahead:
                        project(s + 1, 1 - h, 0, u + 2, range(1, 3), True)
            over_batches(pe, batch)
            out_project(STEPS - 1, 1, range(TT_), False)

        @block.vector
        def _(dve):
            def stats(s, h, x_count, old):
                dve.wait_ge(x_loaded[h], x_count)
                if old:
                    dve.wait_ge(xn_ready, s * 4)
                for t in range(TT_):
                    nc.vector.bn_stats(bn6[:, t], xin[:, h, t]).then_inc(bn_ready, 1)

            def aggregate():
                for t in range(TT_):
                    nc.vector.bn_aggr(mv[:, t], bn6[:, t]).then_inc(mv_ready, 1)

            def neg_mean_rstd(s):
                dve.wait_ge(mv_ready, s * 4 + 4)
                dve.wait_ge(rstd_ready, s + 1)
                nc.vector.scalar_tensor_tensor(out=nmr[:], in0=mv[:, :, 0], scalar=-1.0, in1=rstd[:],
                                               op0=ALU.mult, op1=ALU.mult).then_inc(nmr_ready, 1)

            def shift(s, h, first_step, stats_after):
                if not first_step:
                    dve.wait_ge(mix_ready, s * 12)
                if stats_after is not None:
                    dve.wait_ge(bn_ready, stats_after * 4 + 4)
                if h == 0:
                    nc.vector.memset(hT[:, :, 0], 0.0).then_inc(shift_ready, 1)
                else:
                    dve.wait_ge(hT_ready, s * 4)
                    nc.vector.tensor_copy(hT[:, :, 0], hT[:, :, ST]).then_inc(shift_ready, 1)

            def batch_mod(b, wait_free):
                if wait_free:
                    dve.wait_ge(hT_ready, b * 8)
                nc.vector.tensor_copy(mod[:], per["modT"][:, bass.ds(b, 1), 0:2, :].rearrange("p o q c -> p (o q) c")
                                      ).then_inc(mod_ready, 1)

            def add_shifted(s, h, m):
                for c in range(CT):
                    if m == 0 and c == 0:
                        dve.wait_ge(shift_ready, s + 1)
                    dve.wait_ge(mixprod_ready, s * 12 + 4 * m + c + 1)
                    nc.vector.scalar_tensor_tensor(out=mix[:, h, m, c], in0=hT[:, c, 0:ST],
                                                   scalar=per["one_less_mix"][:, m, c:c + 1], in1=mix[:, h, m, c],
                                                   op0=ALU.mult, op1=ALU.add).then_inc(mix_ready, 1)

            def running_max(u, p, h, q):
                st = state[:, p]
                if h == 0:
                    nc.vector.memset(st[:, 0, :, 0], NEG_HUGE).then_inc(init_ready, 1)
                    nc.vector.memset(st[:, 1:3, :, 0], 0.0).then_inc(init_ready, 1)
                else:
                    nc.vector.tensor_copy(st[:, 0, :, 0], st[:, 0, :, ST]).then_inc(init_ready, 1)
                    nc.vector.tensor_copy(st[:, 1:3, :, 0], st[:, 1:3, :, ST]).then_inc(init_ready, 1)
                dve.wait_ge(k_ready, u + 1)
                dve.wait_ge(init_ready, u * 2 + 2)
                for i in range(2):
                    c = 2 * p + i
                    nc.vector.tensor_tensor_scan(st[:, 0, i, 1:ST + 1], per["w"][:, c:c + 1].to_broadcast([P, ST]),
                                                 kb[:, q, i], st[:, 0, i, 0:1], ALU.add, ALU.max
                                                 ).then_inc(max_ready, 1)
                dve.wait_ge(max_ready, u * 2 + 2)
                nc.vector.tensor_tensor(kp[:], kb[:, q], st[:, 0, :, 0:ST], ALU.subtract).then_inc(kp_ready, 1)

            def states(u, p, q):
                st = state[:, p]
                dve.wait_ge(ha_ready, u + 1)
                dve.wait_ge(e1_ready, u + 1)
                for i in range(2):
                    nc.vector.tensor_tensor_scan(st[:, 2, i, 1:ST + 1], e1[:, i], ha[:, i], st[:, 2, i, 0:1],
                                                 ALU.mult, ALU.add).then_inc(den_state, 1)
                dve.wait_ge(v_ready, u + 1)
                dve.wait_ge(den_state, u * 2 + 2)
                nc.vector.tensor_tensor(ha[:], ha[:], vb[:, q], ALU.mult).then_inc(e2v_ready, 1)
                dve.wait_ge(ga_ready, u + 1)
                dve.wait_ge(gb_ready, u + 1)
                nc.vector.tensor_tensor(kp[:], ga[:], vb[:, q], ALU.mult).then_inc(n2_ready, 1)
                dve.wait_ge(e2v_ready, u + 1)
                for i in range(2):
                    nc.vector.tensor_tensor_scan(st[:, 1, i, 1:ST + 1], e1[:, i], ha[:, i], st[:, 1, i, 0:1],
                                                 ALU.mult, ALU.add).then_inc(num_state, 1)
                dve.wait_ge(num_state, u * 2 + 2)
                nc.vector.tensor_tensor(e1[:], gb[:], st[:, 1, :, 0:ST], ALU.mult).then_inc(n1_ready, 1)
                dve.wait_ge(n1_ready, u + 1)
                nc.vector.tensor_tensor(gb[:], gb[:], st[:, 2, :, 0:ST], ALU.mult).then_inc(d1_ready, 1)
                dve.wait_ge(n2_ready, u + 1)
                dve.wait_ge(d1_ready, u + 1)
                nc.vector.tensor_tensor(ga[:], ga[:], gb[:], ALU.add).then_inc(den_ready, 1)
                dve.wait_ge(eb_ready, u + 1)
                dve.wait_ge(den_ready, u + 1)
                nc.vector.scalar_tensor_tensor(out=ga[:], in0=eb[:, q], scalar=1.0, in1=ga[:], op0=ALU.add,
                                               op1=ALU.mult).then_inc(full_den_ready, 1)
                nc.vector.tensor_tensor(kp[:], kp[:], e1[:], ALU.add).then_inc(num_ready, 1)

            def log_plus_m(u, q):
                dve.wait_ge(log_ready, u + 1)
                dve.wait_ge(m_ready, u + 1)
                nc.vector.tensor_tensor(ga[:], ga[:], mb[:, q], ALU.add).then_inc(logm_ready, 1)

            def output(u, p, h, s, wait_free):
                if wait_free:
                    dve.wait_ge(o_in_psum, s * 4 - 4)
                dve.wait_ge(inv_ready, u + 1)
                dve.wait_ge(num_ready, u + 1)
                nc.vector.tensor_tensor(yT[:, h, 2 * p:2 * p + 2], kp[:], ga[:], ALU.mult).then_inc(y_ready, 1)

            def residual(step, b, ts):
                for t in ts:
                    if t == 0:
                        dve.wait_ge(gate_loaded, b * 16 + 16)
                    dve.wait_ge(o_in_psum, step * 4 + t + 1)
                    nc.vector.tensor_tensor(misc[:, t % 2], misc[:, t % 2], gate[:], ALU.mult).then_inc(gated_ready, 1)
                    dve.wait_ge(gated_ready, step * 4 + t + 1)
                    dve.wait_ge(xres_loaded, step * 16 + 16)
                    nc.vector.tensor_tensor(xres[:, t], misc[:, t % 2], xres[:, t], ALU.add).then_inc(res_ready, 1)

            def transposed_weights(m):
                for c in range(1, CT, 2):
                    dve.wait_ge(wt_in_psum, 4 * m + c + 1)
                    nc.vector.tensor_copy(per["wT"][:, m, c, :], proj[2][:, 1]).then_inc(wt_odd, 1)

            def modulation_rows(ps, first_row, done):
                for q in range(2):
                    nc.vector.tensor_scalar(per["modT"][:, :, first_row + q, :].rearrange("p b c -> p c b"), ps[:, q],
                                            1.0 - q, None, ALU.add).then_inc(done, 1)

            dve.wait_ge(chan_in_psum, 1)
            nc.vector.tensor_copy(per["chan"][:].rearrange("p i c -> p (i c)"), chan_ps).then_inc(chan_ready, 1)
            dve.wait_ge(c_exp_ready, 1)
            nc.vector.tensor_scalar(silu_den[:], silu_exp[:], 1.0, None, ALU.add).then_inc(silu_step, 1)
            dve.wait_ge(silu_step, 1)
            nc.vector.reciprocal(silu_rec[:], silu_den[:]).then_inc(silu_step, 1)
            dve.wait_ge(silu_step, 2)
            nc.vector.tensor_tensor(siluT[:], cT_ps, silu_rec[:], ALU.mult).then_inc(silu_step, 1)
            dve.wait_ge(chan_ready, 1)
            nc.vector.tensor_scalar(per["one_less_mix"][:], per["chan"][:, 0:3, :], -1.0, 1.0, ALU.mult, ALU.add
                                    ).then_inc(const_ready, 1)
            nc.vector.tensor_scalar(per["neg_u"][:], per["chan"][:, 4, :], -1.0, None, ALU.mult
                                    ).then_inc(const_ready, 1)
            dve.wait_ge(decay_ready, 1)
            nc.vector.tensor_scalar(per["w"][:], per["neg_w"][:], -1.0, None, ALU.mult).then_inc(const_ready, 1)
            stats(0, 0, 16, False)
            shift(0, 0, True, 0)
            aggregate()
            neg_mean_rstd(0)
            dve.wait_ge(mod1_in_psum, 1)
            modulation_rows(mod1_ps, SCALE1, mod1_ready)
            dve.wait_ge(mod1_ready, 2)
            batch_mod(0, False)
            dve.wait_ge(const_ready, 3)
            add_shifted(0, 0, 0)
            transposed_weights(0)
            transposed_weights(1)
            add_shifted(0, 0, 1)
            transposed_weights(2)
            add_shifted(0, 0, 2)
            transposed_weights(3)
            stats(1, 1, 16, True)
            dve.wait_ge(bn_ready, 8)
            aggregate()
            neg_mean_rstd(1)
            running_max(0, 0, 0, 0)
            dve.wait_ge(mod2_in_psum, 1)
            g = [g_work[:, i] for i in range(6)]
            modulation_rows(mod2_ps, SCALE2, mod2_ready)
            nc.vector.tensor_copy(g[0], gT_ps).then_inc(g_step, 1)
            dve.wait_ge(g_step, 1)
            nc.vector.tensor_scalar(g[1], g[0], -1.0, None, ALU.mult).then_inc(g_step, 1)
            nc.vector.tensor_scalar(g[2], g[0], 0.0, 2.0, ALU.is_ge, ALU.mult).then_inc(g_step, 1)
            dve.wait_ge(g_step, 3)
            nc.vector.tensor_tensor(g[3], g[0], g[1], ALU.max).then_inc(g_step, 1)
            dve.wait_ge(g_step, 4)
            nc.vector.tensor_scalar(g[4], g[3], GATE_FLOOR, None, ALU.max).then_inc(g_floor, 1)
            dve.wait_ge(g_floor, 1)
            nc.vector.scalar_tensor_tensor(out=g[5], in0=g[2], scalar=1.0, in1=g[4], op0=ALU.subtract, op1=ALU.mult
                                           ).then_inc(g_step, 1)
            dve.wait_ge(gate_rows_in_psum, 1)
            for i in range(2):
                nc.vector.tensor_copy(gate_rows[:, i], misc[0:B, 1 - i, :]).then_inc(gate_rows_ready, 1)

            def batch(b, first, last):
                for h in range(2):
                    s = b * 2 + h
                    u = b * 4 + 2 * h
                    ahead = not (last and h == 1)
                    behind = not (first and h == 0)
                    if not last:
                        stats(s + 2, h, b * 16 + 32, True)
                    if ahead:
                        if h == 1:
                            batch_mod(b + 1, True)
                        shift(s + 1, 1 - h, False, None if last else s + 2)
                    if not last:
                        aggregate()
                    states(u, 0, 0)
                    if ahead:
                        add_shifted(s + 1, 1 - h, 0)
                    log_plus_m(u, 0)
                    if ahead:
                        add_shifted(s + 1, 1 - h, 1)
                    output(u, 0, h, s, not first)
                    running_max(u + 1, 1, h, 1)
                    if not last:
                        neg_mean_rstd(s + 2)
                    if ahead:
                        add_shifted(s + 1, 1 - h, 2)
                    if behind:
                        residual(s - 1, b - 1 + h, range(0, 2))
                    states(u + 1, 1, 1)
                    if behind:
                        residual(s - 1, b - 1 + h, range(2, 3))
                    log_plus_m(u + 1, 1)
                    if behind:
                        residual(s - 1, b - 1 + h, range(3, 4))
                    output(u + 1, 1, h, s, not first)
                    if ahead:
                        running_max(u + 2, 0, 1 - h, 0)
            over_batches(dve, batch)
            residual(STEPS - 1, B - 1, range(TT_))


def ffn(nc, io, per, out):
    with ExitStack() as ctx:
        def sb(name, shape, dt=F32):
            return ctx.enter_context(nc.sbuf_tensor(name, shape, dt))

        def sem(name):
            return ctx.enter_context(nc.semaphore(name))

        xT_hi = sb("xT_hi", [P, CT, NTOK], F32R)
        xT_lo = sb("xT_lo", [P, CT, NTOK], F32R)
        w1_hi = sb("w1_hi", [P, 2, CT, FT * P], F32R)
        w1_lo = sb("w1_lo", [P, 2, CT, FT * P], F32R)
        w2_hi = sb("w2_hi", [P, 2, FT, C], F32R)
        w2_lo = sb("w2_lo", [P, 2, FT, C], F32R)
        wraw = sb("ffn_wraw", [P, CT, C])
        y = sb("y", [P, TOKT, C])
        h_raw = sb("h_raw", [P, 2, ST])
        h_hi = sb("h_hi", [P, 2, FT, ST], F32R)
        h_lo = sb("h_lo", [P, 2, FT, ST], F32R)
        bn6 = sb("ffn_bn6", [P, TOKT, 6])
        mv = sb("ffn_mv", [P, TOKT, 2])
        lnv = sb("ffn_lnv", [P, TOKT])
        rstd = sb("ffn_rstd", [P, TOKT])
        nmr = sb("ffn_nmr", [P, TOKT])
        ew = sb("ew", [P, TOKT, 2])
        wsum = sb("wsum", [P, TOKT])
        gate, x1 = wraw[:, 0:2], wraw[:, 2:4]
        up = ctx.enter_context(nc.psum_tensor("up", [P, FT, ST], F32))
        down = ctx.enter_context(nc.psum_tensor("down", [P, TT_, C], F32))

        x_loaded = [sem(f"ffn_x_loaded{c}") for c in range(CHUNKS)]
        ew_loaded = sem("ew_loaded")
        gates_loaded = sem("gates_loaded")
        wraw_loaded = [sem("w1_loaded"), sem("w2_loaded")]
        bn_ready = sem("ffn_bn_ready")
        mv_ready = sem("ffn_mv_ready")
        lnv_ready = sem("ffn_lnv_ready")
        rstd_ready = sem("ffn_rstd_ready")
        nmr_ready = sem("ffn_nmr_ready")
        xn_ready = sem("ffn_xn_ready")
        xnT_in_psum = sem("ffn_xnT_in_psum")
        xT_ready = sem("ffn_xT_ready")
        xhi_ready = sem("xhi_ready")
        xlo_ready = sem("xlo_ready")
        wsum_ready = sem("wsum_ready")
        zero_ready = sem("y_zeroed")
        whi_ready = [sem("w1_hi_ready"), sem("w2_hi_ready")]
        wlo_ready = [sem("w1_lo_ready"), sem("w2_lo_ready")]
        h_in_psum = sem("h_in_psum")
        gelu_ready = sem("gelu_ready")
        hhi_ready = sem("hhi_ready")
        hlo_ready = sem("hlo_ready")
        y_in_psum = sem("y_in_psum")
        y_ready = sem("ffn_y_ready")
        x1_loaded = [sem("x1_loaded0"), sem("x1_loaded1")]
        scaled_ready = sem("scaled_ready")
        sum_ready = sem("sum_ready")
        final_stored = [sem("final_stored0"), sem("final_stored1")]

        rows = out[0:NTOK, :].rearrange("(n p) c -> p n c", p=P)
        w_rows = [io["w1"].rearrange("(c p) (g n) -> g p c n", p=P, n=FT * P),
                  io["w2"].rearrange("(g f p) n -> g p f n", f=FT, p=P)]
        w_hi, w_lo = (w1_hi, w2_hi), (w1_lo, w2_lo)
        block = ctx.enter_context(nc.Block())
        JOBS = 2 * CHUNKS
        TURNS = GROUPS // 2

        def over_turns(eng, turn):
            turn(0, True, False)
            with eng.Fori(1, TURNS - 1) as it:
                turn(it, False, False)
            turn(TURNS - 1, False, True)

        @block.sync
        def _(sp):
            sp.dma_start(y[:, 0:4], rows[:, 0:4]).then_inc(x_loaded[0], 16)
            sp.dma_start(wraw[:], w_rows[0][0]).then_inc(wraw_loaded[0], 16)
            for c in range(1, CHUNKS):
                sp.dma_start(y[:, 4 * c:4 * c + 4], rows[:, 4 * c:4 * c + 4]).then_inc(x_loaded[c], 16)
            sp.wait_ge(wlo_ready[0], 2)
            sp.dma_start(wraw[:], w_rows[1][0]).then_inc(wraw_loaded[1], 16)
            sp.dma_start(ew[:], io["ew"].rearrange("(n p) k -> p n k", p=P)).then_inc(ew_loaded, 16)
            with sp.Fori(1, GROUPS) as g:
                for i in range(2):
                    if i == 0:
                        sp.wait_ge(wlo_ready[1], g * 2)
                    else:
                        sp.wait_ge(wlo_ready[0], g * 2 + 2)
                    sp.dma_start(wraw[:], w_rows[i][bass.ds(g, 1)].rearrange("o p c n -> (o p) c n")
                                 ).then_inc(wraw_loaded[i], 16)
            sp.wait_ge(wlo_ready[1], GROUPS * 2)
            for b in range(2):
                sp.dma_start(gate[:, b], per["gates"][1, b:b + 1, :].to_broadcast([P, C])).then_inc(gates_loaded, 16)
            for n in range(TOKT + 1):
                if n < TOKT:
                    if n >= 2:
                        sp.wait_ge(final_stored[n % 2], n // 2 * 16)
                    sp.dma_start(x1[:, n % 2], rows[:, n]).then_inc(x1_loaded[n % 2], 16)
                if n >= 1:
                    sp.wait_ge(sum_ready, n)
                    sp.dma_start(rows[:, n - 1], x1[:, (n - 1) % 2]).then_inc(final_stored[(n - 1) % 2], 16)
            for i in range(2):
                sp.wait_ge(final_stored[i], TOKT // 2 * 16)

        @block.scalar
        def _(act):
            def split_weights(g, q, i):
                act.wait_ge(wraw_loaded[i], g * 16 + 16)
                for k in range(2):
                    nc.scalar.activation(w_hi[i][:, q, 2 * k:2 * k + 2], wraw[:, 2 * k:2 * k + 2], ACT.Copy
                                         ).then_inc(whi_ready[i], 1)

            def gelu(job, q, raw_used, half_used):
                for f in range(FT):
                    act.wait_ge(h_in_psum, job * 4 + f + 1)
                    if raw_used or f >= 2:
                        act.wait_ge(hlo_ready, job * 4 - 1 + f)
                    nc.scalar.activation(h_raw[:, f % 2], up[:, f], ACT.Gelu_apprx_tanh).then_inc(gelu_ready, 1)
                    act.wait_ge(gelu_ready, job * 4 + f + 1)
                    if f == 0 and half_used:
                        act.wait_ge(y_in_psum, job * 4 - 4)
                    nc.scalar.activation(h_hi[:, q, f], h_raw[:, f % 2], ACT.Copy).then_inc(hhi_ready, 1)

            def chunk_rstd(c):
                ts = slice(4 * c, 4 * c + 4)
                act.wait_ge(mv_ready, 4 * c + 4)
                nc.scalar.activation(lnv[:, ts], mv[:, ts, 1], ACT.Ln, bias=per["eps"][:, 0:1]).then_inc(lnv_ready, 1)
                act.wait_ge(lnv_ready, c + 1)
                nc.scalar.activation(rstd[:, ts], lnv[:, ts], ACT.Exp, scale=-0.5).then_inc(rstd_ready, 1)

            def chunk_normalise(c):
                act.wait_ge(nmr_ready, c + 1)
                for t in range(4 * c, 4 * c + 4):
                    nc.scalar.activation(y[:, t], y[:, t], ACT.Identity, bias=nmr[:, t:t + 1], scale=rstd[:, t:t + 1]
                                         ).then_inc(xn_ready, 1)

            def chunk_modulate(c):
                for k in range(CT):
                    act.wait_ge(xnT_in_psum, 4 * c + k + 1)
                    if c == 1 and k < 2:
                        act.wait_ge(hlo_ready, 4)
                    elif 4 * c + k >= 2:
                        act.wait_ge(xlo_ready, 4 * c + k - 1)
                    b = c // 2
                    nc.scalar.activation(h_raw[:, k % 2], down[:, k], ACT.Identity,
                                         bias=per["modT"][:, b, SHIFT2, k:k + 1],
                                         scale=per["modT"][:, b, SCALE2, k:k + 1]).then_inc(xT_ready, 1)
                    act.wait_ge(xT_ready, 4 * c + k + 1)
                    nc.scalar.activation(xT_hi[:, k, c * ST:(c + 1) * ST], h_raw[:, k % 2], ACT.Copy
                                         ).then_inc(xhi_ready, 1)

            chunk_rstd(0)
            chunk_normalise(0)
            split_weights(0, 0, 0)
            chunk_modulate(0)
            for c in range(1, CHUNKS):
                chunk_rstd(c)
                chunk_normalise(c)
            act.wait_ge(xlo_ready, 4)
            gelu(0, 0, False, False)
            chunk_modulate(1)
            split_weights(0, 0, 1)
            chunk_modulate(2)
            chunk_modulate(3)
            act.wait_ge(xlo_ready, 4 * CHUNKS)

            def turn(it, first, last):
                for j in range(JOBS):
                    job = it * JOBS + j
                    if not (last and j == JOBS - 1):
                        gelu(job + 1, (j + 1) % 2, True, not (first and j == 0))
                    if j % CHUNKS in (1, 2) and not (last and j > CHUNKS):
                        g = it * 2 + j // CHUNKS
                        if j % CHUNKS == 1 and not (first and j == 1):
                            act.wait_ge(y_in_psum, g * 16)
                        split_weights(g + 1, (j // CHUNKS + 1) % 2, j % CHUNKS - 1)
            over_turns(act, turn)

        @block.gpsimd
        def _(pool):
            for c in range(CHUNKS):
                pool.wait_ge(xnT_in_psum, 4 * c + 4)
                pool.memset(y[:, 4 * c:4 * c + 4], 0.0).then_inc(zero_ready, 1)

        @block.tensor
        def _(pe):
            def first_product(job, g, q, chunk, prologue, group0):
                if group0:
                    pe.wait_ge(xlo_ready, 4 * chunk + 4)
                pe.wait_ge(wlo_ready[0], g * 2 + 2)
                for f in range(FT):
                    if not prologue:
                        pe.wait_ge(gelu_ready, job * 4 - 3 + f)
                    fs, ts = slice(f * P, (f + 1) * P), slice(chunk * ST, (chunk + 1) * ST)
                    for c in range(CT):
                        hi, lo = w1_hi[:, q, c, fs], w1_lo[:, q, c, fs]
                        nc.tensor.matmul(up[:, f], hi, xT_hi[:, c, ts], start=(c == 0), stop=False)
                        nc.tensor.matmul(up[:, f], hi, xT_lo[:, c, ts], start=False, stop=False)
                        last = nc.tensor.matmul(up[:, f], lo, xT_hi[:, c, ts], start=False, stop=(c == CT - 1))
                    last.then_inc(h_in_psum, 1)

            def second_product(job, g, q, hq, old):
                pe.wait_ge(hlo_ready, job * 4 + 4)
                pe.wait_ge(wlo_ready[1], g * 2 + 2)
                for t in range(TT_):
                    if old:
                        pe.wait_ge(y_ready, job * 4 - 3 + t)
                    else:
                        pe.wait_ge(xT_ready, 4 * CHUNKS)
                    ts = slice(t * P, (t + 1) * P)
                    for f in range(FT):
                        hi, lo = h_hi[:, hq, f, ts], h_lo[:, hq, f, ts]
                        nc.tensor.matmul(down[:, t], hi, w2_hi[:, q, f], start=(f == 0), stop=False)
                        nc.tensor.matmul(down[:, t], hi, w2_lo[:, q, f], start=False, stop=False)
                        last = nc.tensor.matmul(down[:, t], lo, w2_hi[:, q, f], start=False, stop=(f == FT - 1))
                    last.then_inc(y_in_psum, 1)

            def chunk_transposes(c):
                pe.wait_ge(xn_ready, 4 * c + 4)
                for k in range(CT):
                    if c >= 1:
                        pe.wait_ge(xT_ready, 4 * c - 3 + k)
                    for t in range(TT_):
                        last = nc.tensor.transpose(down[:, k, t * P:(t + 1) * P], y[:, 4 * c + t, k * P:(k + 1) * P],
                                                   per["ident"][:])
                    last.then_inc(xnT_in_psum, 1)

            chunk_transposes(0)
            first_product(0, 0, 0, 0, True, True)
            for c in range(1, CHUNKS):
                chunk_transposes(c)

            def turn(it, first, last):
                for j in range(JOBS):
                    job = it * JOBS + j
                    n = j + 1
                    if not (last and j == JOBS - 1):
                        first_product(job + 1, it * 2 + n // CHUNKS, (n // CHUNKS) % 2, n % CHUNKS, False,
                                      first and n < CHUNKS)
                    second_product(job, it * 2 + j // CHUNKS, j // CHUNKS, j % 2, not (first and j == 0))
            over_turns(pe, turn)

        @block.vector
        def _(dve):
            def split_rest(g, q, i):
                for k in range(2):
                    dve.wait_ge(whi_ready[i], g * 2 + k + 1)
                    nc.vector.tensor_tensor(w_lo[i][:, q, 2 * k:2 * k + 2], wraw[:, 2 * k:2 * k + 2],
                                            w_hi[i][:, q, 2 * k:2 * k + 2], ALU.subtract
                                            ).then_inc(wlo_ready[i], 1)

            def h_rest(job, q, half_used):
                for f in range(FT):
                    dve.wait_ge(hhi_ready, job * 4 + f + 1)
                    if f == 0 and half_used:
                        dve.wait_ge(y_in_psum, job * 4 - 4)
                    nc.vector.tensor_tensor(h_lo[:, q, f], h_raw[:, f % 2], h_hi[:, q, f], ALU.subtract
                                            ).then_inc(hlo_ready, 1)

            def accumulate(job, chunk, old):
                for t in range(TT_):
                    n = chunk * TT_ + t
                    dve.wait_ge(y_in_psum, job * 4 + t + 1)
                    if old:
                        dve.wait_ge(y_ready, job * 4 - 4 * CHUNKS + t + 1)
                    nc.vector.tensor_tensor(y[:, n], down[:, t], y[:, n], ALU.add).then_inc(y_ready, 1)

            def chunk_stats(c):
                ts = slice(4 * c, 4 * c + 4)
                dve.wait_ge(x_loaded[c], 16)
                for t in range(4 * c, 4 * c + 4):
                    nc.vector.bn_stats(bn6[:, t], y[:, t]).then_inc(bn_ready, 1)
                for t in range(4 * c, 4 * c + 4):
                    dve.wait_ge(bn_ready, t + 1)
                    nc.vector.bn_aggr(mv[:, t], bn6[:, t]).then_inc(mv_ready, 1)
                dve.wait_ge(mv_ready, 4 * c + 4)
                dve.wait_ge(rstd_ready, c + 1)
                nc.vector.scalar_tensor_tensor(out=nmr[:, ts], in0=mv[:, ts, 0], scalar=-1.0, in1=rstd[:, ts],
                                               op0=ALU.mult, op1=ALU.mult).then_inc(nmr_ready, 1)

            def chunk_rest(c):
                for k in range(CT):
                    dve.wait_ge(xhi_ready, 4 * c + k + 1)
                    cs = slice(c * ST, (c + 1) * ST)
                    nc.vector.tensor_tensor(xT_lo[:, k, cs], h_raw[:, k % 2], xT_hi[:, k, cs], ALU.subtract
                                            ).then_inc(xlo_ready, 1)

            chunk_stats(0)
            split_rest(0, 0, 0)
            chunk_rest(0)
            for c in range(1, CHUNKS):
                chunk_stats(c)
            h_rest(0, 0, False)
            chunk_rest(1)
            split_rest(0, 0, 1)
            chunk_rest(2)
            chunk_rest(3)
            dve.wait_ge(ew_loaded, 16)
            nc.vector.tensor_tensor(wsum[:], ew[:, :, 0], ew[:, :, 1], ALU.add).then_inc(wsum_ready, 1)
            dve.wait_ge(zero_ready, CHUNKS)

            def finish(chunk):
                if chunk == 0:
                    dve.wait_ge(gates_loaded, 32)
                    dve.wait_ge(wsum_ready, 1)
                for n in range(4 * chunk, 4 * chunk + 4):
                    dve.wait_ge(y_ready, (GROUPS - 1) * CHUNKS * 4 + n + 1)
                    nc.vector.scalar_tensor_tensor(out=y[:, n], in0=y[:, n], scalar=wsum[:, n:n + 1],
                                                   in1=gate[:, n // (T // P)], op0=ALU.mult, op1=ALU.mult
                                                   ).then_inc(scaled_ready, 1)
                for n in range(4 * chunk, 4 * chunk + 4):
                    dve.wait_ge(scaled_ready, n + 1)
                    dve.wait_ge(x1_loaded[n % 2], n // 2 * 16 + 16)
                    nc.vector.tensor_tensor(x1[:, n % 2], y[:, n], x1[:, n % 2], ALU.add).then_inc(sum_ready, 1)

            def turn(it, first, last):
                for j in range(JOBS):
                    job = it * JOBS + j
                    if not (last and j == JOBS - 1):
                        h_rest(job + 1, (j + 1) % 2, not (first and j == 0))
                    accumulate(job, j % CHUNKS, not (first and j < CHUNKS))
                    if last and j >= CHUNKS:
                        finish(j - CHUNKS)
                    if j % CHUNKS in (1, 2) and not (last and j > CHUNKS):
                        split_rest(it * 2 + j // CHUNKS + 1, (j // CHUNKS + 1) % 2, j % CHUNKS - 1)
            over_turns(dve, turn)


def adaln_rwkv_ffn(nc, io, out):
    with ExitStack() as ctx:
        def sb(name, shape, dt=F32):
            return ctx.enter_context(nc.sbuf_tensor(name, shape, dt))

        scratch = {"gates": nc.dram_tensor("gates", (2, B, C), F32, kind="Internal").ap()}
        per = {
            "ident": sb("ident", [P, P]),
            "eps": sb("eps", [P, 1]),
            "chan": sb("chan", [P, 5, CT]),
            "one_less_mix": sb("one_less_mix", [P, 3, CT]),
            "neg_w": sb("neg_w", [P, CT]),
            "w": sb("w", [P, CT]),
            "neg_u": sb("neg_u", [P, CT]),
            "modT": sb("modT", [P, B, 4, CT]),
            "gates": scratch["gates"],
        }
        with ExitStack() as attention_only:
            per["wT"] = attention_only.enter_context(nc.sbuf_tensor("wT", [P, 4, CT, C], F32))
            attention(nc, io, per, scratch, out)
        ffn(nc, io, per, out)


_INS = {
    "L0_attn_x": "x", "L0_attn_time_decay": "decay", "L0_attn_time_first": "first", "L0_attn_time_mix_k": "mix_k",
    "L0_attn_time_mix_v": "mix_v", "L0_attn_time_mix_r": "mix_r", "L0_attn_Wk": "Wk", "L0_attn_Wv": "Wv",
    "L0_attn_Wr": "Wr", "L0_attn_Wo": "Wo", "L0_ffn_expert_weights": "ew", "L0_ffn_w1": "w1", "L0_ffn_w2": "w2",
    "L0_c": "c", "L0_wmod": "wmod",
}


def kernel(**inputs):
    import numpy as _np
    import concourse.bacc as _bacc
    from concourse import mybir as _mybir
    from concourse.bass_utils import run_bass_kernel_spmd as _run

    nc = _bacc.Bacc("TRN2", target_bir_lowering=False, num_devices=1, dynamic_dma_scratch_size=1024)
    arrays, io = {}, {}
    for name, short in _INS.items():
        a = _np.ascontiguousarray(inputs[name])
        if short == "x":
            a = a.reshape(B * T, C)
        if short.startswith("mix"):
            a = a.reshape(C)
        arrays[f"in_{short}"] = a
        io[short] = nc.dram_tensor(f"in_{short}", a.shape, _mybir.dt.from_np(a.dtype), kind="ExternalInput").ap()
    out = nc.dram_tensor("out_0", (B * T, C), _mybir.dt.float32, kind="ExternalOutput").ap()
    adaln_rwkv_ffn(nc, io, out)
    r = _run(nc, [arrays], core_ids=[0])
    return r.results[0]["out_0"].reshape(B, T, C)
```

```python
from contextlib import ExitStack

import concourse.bass as bass
from concourse import mybir

P = 128
F32 = mybir.dt.float32
F32R = mybir.dt.float32r
ALU = mybir.AluOpType
ACT = mybir.ActivationFunctionType

EPS = 1e-5
LN_EXP_SET = 6
NEG_HUGE = -1e38
GATE_FLOOR = 0.25

B, T, C = 8, 1024, 512
CT = C // P
ST = 512
TT_ = ST // P
STEPS = B * T // ST
NTOK = 2048
FT = 4
FH = 4096
GROUPS = FH // (FT * P)
CHUNKS = NTOK // ST
TOKT = NTOK // P
MK, MV, MR, MO = range(4)
SPLIT = 2
SCALE1, SHIFT1, SCALE2, SHIFT2 = range(4)


def attention(nc, io, per, scratch, out):
    with ExitStack() as ctx:
        def sb(name, shape, dt=F32):
            return ctx.enter_context(nc.sbuf_tensor(name, shape, dt))

        def sem(name):
            return ctx.enter_context(nc.semaphore(name))

        xin = sb("xin", [P, 2, TT_, C])
        xres = sb("xres", [P, TT_, C])
        gate = sb("gate", [P, C])
        bn6 = sb("bn6", [P, TT_, 6])
        mv = sb("mv", [P, TT_, 2])
        lnv = sb("lnv", [P, TT_])
        rstd = sb("rstd", [P, TT_])
        nmr = sb("nmr", [P, TT_])
        mod = sb("mod", [P, 2, CT])
        hT = sb("hT", [P, CT, ST + 1])
        mix_hi = sb("mix_hi", [P, SPLIT, CT, ST], F32R)
        mix_lo = sb("mix_lo", [P, SPLIT, CT, ST], F32R)
        whole = sb("whole", [P, 2, CT, ST])
        mix = [whole[:, 0], whole[:, 1], whole[:, 1]]
        state = sb("state", [P, 2, 3, 2, ST + 1])
        k_bufs = sb("k_bufs", [P, 2, 2, ST])
        kb, kp = k_bufs[:, 0], k_bufs[:, 1]
        vb = sb("vb", [P, 2, 2, ST])
        mb = sb("mb", [P, 2, 2, ST])
        eb = sb("eb", [P, 2, 2, ST])
        ha = sb("ha", [P, 2, ST])
        e1 = sb("e1", [P, 2, ST])
        out_weights = sb("out_weights", [P, 2, 2, ST])
        ga, gb = out_weights[:, 0], out_weights[:, 1]
        yT = sb("yT", [P, 2, CT, ST])
        proj = [ctx.enter_context(nc.psum_tensor(f"proj{m}", [P, 2, ST], F32)) for m in range(3)]
        misc = ctx.enter_context(nc.psum_tensor("misc", [P, 2, ST], F32))

        c_in = gate[0:B, :]
        chan_rows = e1[0:5 * CT, 0, 0:P]
        w_raw = [t[:].rearrange("p a b c -> p (a b) c") for t in (k_bufs, vb, mb, eb)]
        wmod1 = whole[:].rearrange("p m c t -> p (m c t)").rearrange("p (k n) -> p k n", k=CT)
        wmod_ga = out_weights[:].rearrange("p g i t -> p (g i) t")
        wmod2 = yT[:].rearrange("p h c t -> p (h c t)").rearrange("p (k n) -> p k n", k=CT)
        wmod_gb = xres
        gate_rows = xres[0:B, 0:2, :]
        pair1 = state[:, 1].rearrange("p a i t -> p (a i t)")
        silu_exp, silu_den, silu_rec, siluT = (
            pair1[:, i * CT * B:(i + 1) * CT * B].rearrange("p (c b) -> p c b", c=CT) for i in range(4))
        g_work = pair1[:, 4 * CT * B:16 * CT * B].rearrange("p (i g c b) -> p i g c b", i=6, g=2, c=CT)
        chan_ps = misc[:, 0, 0:5 * CT]
        cT_ps = misc[:, 1, 0:CT * B].rearrange("p (k b) -> p k b", k=CT)
        mod1_ps = proj[1][:, 1, 0:2 * CT * B].rearrange("p (q c b) -> p q c b", q=2, c=CT)
        mod2_ps = misc[:, 0, 0:2 * CT * B].rearrange("p (q c b) -> p q c b", q=2, c=CT)
        gT_ps = misc[:, 0, 64:64 + 2 * CT * B].rearrange("p (g c b) -> p g c b", g=2, c=CT)

        c_loaded = sem("c_loaded")
        chan_loaded = sem("chan_loaded")
        w_loaded = [sem(f"w_loaded{m}") for m in range(4)]
        wmod1_loaded = sem("wmod1_loaded")
        wmod_ga_loaded = sem("wmod_ga_loaded")
        wmod2_loaded = sem("wmod2_loaded")
        wmod_gb_loaded = sem("wmod_gb_loaded")
        ident_zero = sem("ident_zero")
        ident_ready = sem("ident_ready")
        eps_ready = sem("eps_ready")
        chan_in_psum = sem("chan_in_psum")
        chan_ready = sem("chan_ready")
        const_ready = sem("const_ready")
        decay_ready = sem("decay_ready")
        cT_in_psum = sem("cT_in_psum")
        c_exp_ready = sem("c_exp_ready")
        silu_step = sem("silu_step")
        mod1_in_psum = sem("mod1_in_psum")
        mod1_ready = sem("mod1_ready")
        mod2_in_psum = sem("mod2_in_psum")
        g_floor = sem("g_floor")
        g_step = sem("g_step")
        mod2_ready = sem("mod2_ready")
        gate_rows_in_psum = sem("gate_rows_in_psum")
        gate_rows_ready = sem("gate_rows_ready")
        gates_stored = sem("gates_stored")
        wt_in_psum = sem("wt_in_psum")
        wt_hi_ready = sem("wt_hi_ready")
        wt_lo_ready = sem("wt_lo_ready")
        wt_even = sem("wt_even")
        wt_odd = sem("wt_odd")

        x_loaded = [sem("x_loaded0"), sem("x_loaded1")]
        xres_loaded = sem("xres_loaded")
        gate_loaded = sem("gate_loaded")
        out_stored = sem("out_stored")
        mod_ready = sem("mod_ready")
        bn_ready = sem("bn_ready")
        mv_ready = sem("mv_ready")
        lnv_ready = sem("lnv_ready")
        rstd_ready = sem("rstd_ready")
        nmr_ready = sem("nmr_ready")
        xn_ready = sem("xn_ready")
        xnT_in_psum = sem("xnT_in_psum")
        shift_ready = sem("shift_ready")
        hT_ready = sem("hT_ready")
        mixprod_ready = sem("mixprod_ready")
        mixsum_ready = sem("mixsum_ready")
        mixhi_ready = sem("mixhi_ready")
        mixlo_ready = sem("mixlo_ready")
        in_psum = [sem("k_in_psum"), sem("v_in_psum"), sem("r_in_psum")]
        k_ready = sem("k_ready")
        v_ready = sem("v_ready")
        m_ready = sem("m_ready")
        absr_ready = sem("absr_ready")
        eb_ready = sem("eb_ready")
        init_ready = sem("init_ready")
        max_ready = sem("max_ready")
        kp_ready = sem("kp_ready")
        e1_arg = sem("e1_arg")
        ha_arg = sem("ha_arg")
        ga_arg = sem("ga_arg")
        gb_arg = sem("gb_arg")
        e1_ready = sem("e1_ready")
        ha_ready = sem("ha_ready")
        ga_ready = sem("ga_ready")
        gb_ready = sem("gb_ready")
        den_state = sem("den_state")
        e2v_ready = sem("e2v_ready")
        num_state = sem("num_state")
        n2_ready = sem("n2_ready")
        n1_ready = sem("n1_ready")
        d1_ready = sem("d1_ready")
        den_ready = sem("den_ready")
        full_den_ready = sem("full_den_ready")
        log_ready = sem("log_ready")
        logm_ready = sem("logm_ready")
        inv_ready = sem("inv_ready")
        num_ready = sem("num_ready")
        y_ready = sem("y_ready")
        o_in_psum = sem("o_in_psum")
        gated_ready = sem("gated_ready")
        res_ready = sem("res_ready")

        x_rows = io["x"].rearrange("(s t p) c -> s p t c", t=TT_, p=P)
        out_rows = out.rearrange("(s t p) c -> s p t c", t=TT_, p=P)
        block = ctx.enter_context(nc.Block())

        def over_batches(eng, batch):
            batch(0, first=True, last=False)
            with eng.Fori(1, B - 1) as b:
                batch(b, first=False, last=False)
            batch(B - 1, first=False, last=True)

        @block.sync
        def _(sp):
            def load_x(b, h):
                s = b * 2 + h
                sp.dma_start(xin[:, h], x_rows[bass.ds(s, 1)].rearrange("o p t c -> (o p) t c")
                             ).then_inc(x_loaded[h], 16)

            def residual(b, h, step, wait_stored):
                if wait_stored:
                    sp.wait_ge(out_stored, step * 16)
                sp.dma_start(xres[:], x_rows[bass.ds(step, 1)].rearrange("o p t c -> (o p) t c")
                             ).then_inc(xres_loaded, 16)
                if h == 0:
                    if wait_stored:
                        sp.wait_ge(gated_ready, step * 4)
                    sp.dma_start(gate[:], scratch["gates"][0, bass.ds(b, 1), :].to_broadcast([P, C])
                                 ).then_inc(gate_loaded, 16)
                sp.wait_ge(res_ready, step * 4 + 4)
                sp.dma_start(out_rows[bass.ds(step, 1)].rearrange("o p t c -> (o p) t c"), xres[:]
                             ).then_inc(out_stored, 16)

            sp.dma_start(c_in, io["c"]).then_inc(c_loaded, 16)
            for i, name in enumerate(("mix_k", "mix_v", "mix_r", "decay", "first")):
                sp.dma_start(chan_rows[i * CT:(i + 1) * CT, :], io[name].rearrange("(c p) -> c p", p=P)
                             ).then_inc(chan_loaded, 16)
            load_x(0, 0)
            wmod_rows = io["wmod"].rearrange("(k p) n -> p k n", p=P)
            sp.dma_start(wmod1, wmod_rows[:, :, 0:2 * C]).then_inc(wmod1_loaded, 16)
            for m, name in enumerate(("Wk", "Wv", "Wr", "Wo")):
                sp.dma_start(w_raw[m], io[name].rearrange("(t p) c -> p t c", p=P)).then_inc(w_loaded[m], 16)
            load_x(0, 1)
            sp.dma_start(wmod_ga, wmod_rows[:, :, 2 * C:3 * C]).then_inc(wmod_ga_loaded, 16)
            sp.dma_start(wmod2, wmod_rows[:, :, 3 * C:5 * C]).then_inc(wmod2_loaded, 16)
            sp.dma_start(wmod_gb[:], wmod_rows[:, :, 5 * C:6 * C]).then_inc(wmod_gb_loaded, 16)
            sp.wait_ge(gate_rows_ready, 2)
            sp.dma_start(scratch["gates"].rearrange("g b c -> b g c"), gate_rows).then_inc(gates_stored, 16)
            sp.wait_ge(gates_stored, 16)

            def batch(b, first, last):
                for h in range(2):
                    s = b * 2 + h
                    if not last:
                        sp.wait_ge(xnT_in_psum, s * 4 + 4)
                        load_x(b + 1, h)
                    if not (first and h == 0):
                        if h == 0:
                            residual(b - 1, 1, s - 1, True)
                        else:
                            residual(b, 0, s - 1, not first)
            over_batches(sp, batch)
            residual(B - 1, 1, STEPS - 1, True)
            sp.wait_ge(out_stored, STEPS * 16)

        @block.gpsimd
        def _(pool):
            pool.memset(per["ident"][:], 0.0).then_inc(ident_zero, 1)
            pool.memset(per["eps"][:], EPS).then_inc(eps_ready, 1)
            pool.wait_ge(ident_zero, 1)
            pool.affine_select(out=per["ident"][:], in_=per["ident"][:], compare_op=ALU.not_equal, fill=1.0, base=0,
                               pattern=[[-1, P]], channel_multiplier=1).then_inc(ident_ready, 1)

        @block.scalar
        def _(act):
            def transposed_weights(m):
                for c in range(0, CT, 1 if m < SPLIT else 2):
                    act.wait_ge(wt_in_psum, 4 * m + c + 1)
                    if m < SPLIT:
                        nc.scalar.activation(per["wT_hi"][:, m, c, :], proj[2][:, c % 2], ACT.Copy
                                             ).then_inc(wt_hi_ready, 1)
                    else:
                        nc.scalar.activation(per["wT"][:, m - SPLIT, c, :], proj[2][:, 0], ACT.Copy
                                             ).then_inc(wt_even, 1)

            def rstd_of(s):
                act.wait_ge(mv_ready, s * 4 + 4)
                nc.scalar.activation(lnv[:], mv[:, :, 1], ACT.Ln, bias=per["eps"][:, 0:1]).then_inc(lnv_ready, 1)
                act.wait_ge(lnv_ready, s + 1)
                nc.scalar.activation(rstd[:], lnv[:], ACT.Exp, scale=-0.5).then_inc(rstd_ready, 1)

            def normalise(s, h):
                act.wait_ge(nmr_ready, s + 1)
                for t in range(TT_):
                    nc.scalar.activation(xin[:, h, t], xin[:, h, t], ACT.Identity, bias=nmr[:, t:t + 1],
                                         scale=rstd[:, t:t + 1]).then_inc(xn_ready, 1)

            def modulate(s, b, cs, first_step):
                act.wait_ge(mod_ready, b + 1)
                act.wait_ge(shift_ready, s + 1)
                if not first_step:
                    act.wait_ge(mixsum_ready, s * 12)
                for c in cs:
                    act.wait_ge(xnT_in_psum, s * 4 + c + 1)
                    nc.scalar.activation(hT[:, c, 1:ST + 1], misc[:, c % 2], ACT.Identity,
                                         bias=mod[:, SHIFT1, c:c + 1], scale=mod[:, SCALE1, c:c + 1]
                                         ).then_inc(hT_ready, 1)

            def mixprods(s, m, cs, old):
                if m == 0 and old:
                    act.wait_ge(mixlo_ready, s * 2 * SPLIT - 2)
                if m == 1 and old:
                    act.wait_ge(in_psum[2], s * 2)
                if m == 2:
                    act.wait_ge(mixlo_ready, s * 2 * SPLIT + 4)
                for c in cs:
                    if m == 0:
                        act.wait_ge(hT_ready, s * 4 + c + 1)
                    nc.scalar.activation(mix[m][:, c], hT[:, c, 1:ST + 1], ACT.Copy,
                                         scale=per["chan"][:, m, c:c + 1]).then_inc(mixprod_ready, 1)

            def mix_leading(s, m, old):
                if old:
                    act.wait_ge(in_psum[m], s * 2)
                for k in range(0, CT, 2):
                    act.wait_ge(mixsum_ready, s * 12 + 4 * m + k + 2)
                    nc.scalar.activation(mix_hi[:, m, k:k + 2], mix[m][:, k:k + 2], ACT.Copy).then_inc(mixhi_ready, 1)

            def evacuate_kv(u, q, m, old):
                act.wait_ge(in_psum[m], u + 1)
                if old and m == 0:
                    act.wait_ge(kp_ready, u)
                if old and m == 1:
                    act.wait_ge(y_ready, u - 1)
                nc.scalar.activation(kb if m == 0 else vb[:, q], proj[m][:], ACT.Copy
                                     ).then_inc(k_ready if m == 0 else v_ready, 1)

            def evacuate_r(u, q, old):
                act.wait_ge(in_psum[2], u + 1)
                if old:
                    act.wait_ge(logm_ready, u - 1)
                nc.scalar.activation(mb[:, q], proj[2][:], ACT.Relu, scale=-1.0).then_inc(m_ready, 1)
                nc.scalar.activation(eb[:, q], proj[2][:], ACT.Abs).then_inc(absr_ready, 1)
                act.wait_ge(absr_ready, u + 1)
                nc.scalar.activation(eb[:, q], eb[:, q], ACT.Exp, scale=-1.0).then_inc(eb_ready, 1)

            def state_weights(u, p):
                act.wait_ge(kp_ready, u + 1)
                for i in range(2):
                    c = 2 * p + i
                    nc.scalar.activation(e1[:, i], kp[:, i], ACT.Relu, bias=per["neg_w"][:, c:c + 1]
                                         ).then_inc(e1_arg, 1)
                    nc.scalar.activation(ha[:, i], kp[:, i], ACT.Relu, bias=per["w"][:, c:c + 1], scale=-1.0
                                         ).then_inc(ha_arg, 1)
                act.wait_ge(e1_arg, u * 2 + 2)
                nc.scalar.activation(e1[:], e1[:], ACT.Exp, scale=-1.0).then_inc(e1_ready, 1)
                act.wait_ge(ha_arg, u * 2 + 2)
                nc.scalar.activation(ha[:], ha[:], ACT.Exp, scale=-1.0).then_inc(ha_ready, 1)

            def output_weights(u, p, old):
                if old:
                    act.wait_ge(y_ready, u)
                for i in range(2):
                    c = 2 * p + i
                    nc.scalar.activation(ga[:, i], kp[:, i], ACT.Relu, bias=per["neg_u"][:, c:c + 1], scale=-1.0
                                         ).then_inc(ga_arg, 1)
                    nc.scalar.activation(gb[:, i], kp[:, i], ACT.Relu, bias=per["chan"][:, 4, c:c + 1]
                                         ).then_inc(gb_arg, 1)
                act.wait_ge(ga_arg, u * 2 + 2)
                nc.scalar.activation(ga[:], ga[:], ACT.Exp, scale=-1.0).then_inc(ga_ready, 1)
                act.wait_ge(gb_arg, u * 2 + 2)
                nc.scalar.activation(gb[:], gb[:], ACT.Exp, scale=-1.0).then_inc(gb_ready, 1)

            def log_den(u):
                act.wait_ge(full_den_ready, u + 1)
                nc.scalar.activation(ga[:], ga[:], ACT.Ln).then_inc(log_ready, 1)

            def inverse(u):
                act.wait_ge(logm_ready, u + 1)
                nc.scalar.activation(ga[:], ga[:], ACT.Exp, scale=-1.0).then_inc(inv_ready, 1)

            act.add_instruction(mybir.InstLoadActFuncSet(name=nc.get_next_instruction_name(),
                                                         act_func_set_id=LN_EXP_SET, ins=[], outs=[]))
            act.wait_ge(cT_in_psum, 1)
            nc.scalar.activation(silu_exp[:], cT_ps, ACT.Exp, scale=-1.0).then_inc(c_exp_ready, 1)
            act.wait_ge(chan_ready, 1)
            nc.scalar.activation(per["neg_w"][:], per["chan"][:, 3, :], ACT.Exp).then_inc(decay_ready, 1)
            act.wait_ge(eps_ready, 1)
            rstd_of(0)
            normalise(0, 0)
            modulate(0, 0, range(CT), True)
            mixprods(0, 0, range(CT), False)
            transposed_weights(0)
            mix_leading(0, 0, False)
            mixprods(0, 1, range(CT), False)
            transposed_weights(1)
            mix_leading(0, 1, False)
            transposed_weights(2)
            mixprods(0, 2, range(CT), False)
            transposed_weights(3)
            evacuate_kv(0, 0, 0, False)
            rstd_of(1)
            normalise(1, 1)
            state_weights(0, 0)
            evacuate_kv(0, 0, 1, False)
            act.wait_ge(mod2_in_psum, 1)
            output_weights(0, 0, False)

            def batch(b, first, last):
                for h in range(2):
                    s = b * 2 + h
                    u = b * 4 + 2 * h
                    ahead = not (last and h == 1)
                    nb = b + h
                    behind = not (first and h == 0)
                    evacuate_r(u, 0, behind)
                    if ahead:
                        modulate(s + 1, nb, range(0, 2), False)
                        mixprods(s + 1, 0, range(0, 2), True)
                    log_den(u)
                    evacuate_kv(u + 1, 1, 0, True)
                    if ahead:
                        modulate(s + 1, nb, range(2, 4), False)
                    inverse(u)
                    if ahead:
                        mixprods(s + 1, 0, range(2, 4), True)
                    state_weights(u + 1, 1)
                    if ahead:
                        mix_leading(s + 1, 0, True)
                    evacuate_kv(u + 1, 1, 1, behind)
                    if ahead:
                        mixprods(s + 1, 1, range(CT), True)
                    output_weights(u + 1, 1, True)
                    if ahead:
                        mix_leading(s + 1, 1, True)
                    if not last:
                        rstd_of(s + 2)
                    evacuate_r(u + 1, 1, behind)
                    if ahead:
                        evacuate_kv(u + 2, 0, 0, True)
                        mixprods(s + 1, 2, range(CT), True)
                    log_den(u + 1)
                    if not last:
                        normalise(s + 2, h)
                    inverse(u + 1)
                    if ahead:
                        state_weights(u + 2, 0)
                        evacuate_kv(u + 2, 0, 1, True)
                        output_weights(u + 2, 0, True)
            over_batches(act, batch)

        @block.tensor
        def _(pe):
            def transposes(s, h, cs, old):
                pe.wait_ge(xn_ready, s * 4 + 4)
                for c in cs:
                    if c >= 2:
                        pe.wait_ge(hT_ready, s * 4 + c - 1)
                    elif old:
                        pe.wait_ge(res_ready, s * 4 - 9 + c)
                    for t in range(TT_):
                        last = nc.tensor.transpose(misc[:, c % 2, t * P:(t + 1) * P], xin[:, h, t, c * P:(c + 1) * P],
                                                   per["ident"][:])
                    last.then_inc(xnT_in_psum, 1)

            def project(s, h, p, u, ms, old):
                for m in ms:
                    if m < SPLIT:
                        pe.wait_ge(mixlo_ready, s * 2 * SPLIT + 2 * m + 2)
                    else:
                        pe.wait_ge(mixsum_ready, s * 12 + 4 * m + 4)
                    if old:
                        pe.wait_ge((k_ready, v_ready, absr_ready)[m], u)
                    for i in range(2):
                        d = 2 * p + i
                        for c in range(CT):
                            if m < SPLIT:
                                hi, lo = (per[w][:, m, c, d * P:(d + 1) * P] for w in ("wT_hi", "wT_lo"))
                                nc.tensor.matmul(proj[m][:, i], hi, mix_hi[:, m, c], start=(c == 0), stop=False)
                                nc.tensor.matmul(proj[m][:, i], hi, mix_lo[:, m, c], start=False, stop=False)
                                last = nc.tensor.matmul(proj[m][:, i], lo, mix_hi[:, m, c], start=False,
                                                        stop=(c == CT - 1))
                            else:
                                last = nc.tensor.matmul(proj[m][:, i], per["wT"][:, m - SPLIT, c, d * P:(d + 1) * P],
                                                        mix[m][:, c], start=(c == 0), stop=(c == CT - 1))
                    last.then_inc(in_psum[m], 1)

            def out_project(s, h, ts, ahead):
                pe.wait_ge(y_ready, s * 2 + 2)
                for t in ts:
                    if t >= 2:
                        pe.wait_ge(res_ready, s * 4 + t - 1)
                    elif ahead:
                        pe.wait_ge(hT_ready, s * 4 + 8 + t + 3)
                    else:
                        pe.wait_ge(res_ready, s * 4 - 1 + t)
                    for c in range(CT):
                        last = nc.tensor.matmul(misc[:, t % 2], yT[:, h, c, t * P:(t + 1) * P], per["wT"][:, MO - SPLIT, c, :],
                                                start=(c == 0), stop=(c == CT - 1))
                    last.then_inc(o_in_psum, 1)

            def transpose_weights(m):
                pe.wait_ge(w_loaded[m], 16)
                for c in range(CT):
                    before = 4 * m + c - 2
                    if before >= 4 * SPLIT:
                        pe.wait_ge((wt_even, wt_odd)[c % 2], (before - 4 * SPLIT) // 2 + 1)
                    elif before >= 0:
                        pe.wait_ge(wt_lo_ready, before + 1)
                    for t in range(CT):
                        last = nc.tensor.transpose(proj[2][:, c % 2, t * P:(t + 1) * P],
                                                   w_raw[m][:, t, c * P:(c + 1) * P], per["ident"][:])
                    last.then_inc(wt_in_psum, 1)

            def modulation(dest, w, col):
                for c in range(CT):
                    for k in range(CT):
                        last = nc.tensor.matmul(dest[:, c, :], w[:, k, col * C + c * P:col * C + (c + 1) * P],
                                                siluT[:, k, :], start=(k == 0), stop=(k == CT - 1))
                return last

            pe.wait_ge(ident_ready, 1)
            pe.wait_ge(chan_loaded, 80)
            nc.tensor.transpose(chan_ps, chan_rows, per["ident"][0:5 * CT, 0:5 * CT]).then_inc(chan_in_psum, 1)
            pe.wait_ge(c_loaded, 16)
            for k in range(CT):
                last = nc.tensor.transpose(cT_ps[:, k, :], c_in[:, k * P:(k + 1) * P], per["ident"][0:B, 0:B])
            last.then_inc(cT_in_psum, 1)
            pe.wait_ge(silu_step, 3)
            pe.wait_ge(wmod1_loaded, 16)
            modulation(mod1_ps[:, SCALE1], wmod1, 1)
            modulation(mod1_ps[:, SHIFT1], wmod1, 0).then_inc(mod1_in_psum, 1)
            pe.wait_ge(chan_ready, 1)
            transposes(0, 0, range(CT), False)
            transpose_weights(MK)
            transpose_weights(MV)
            pe.wait_ge(wt_lo_ready, 4)
            project(0, 0, 0, 0, range(0, 1), False)
            transpose_weights(MR)
            pe.wait_ge(wt_lo_ready, 8)
            pe.wait_ge(mod1_ready, 2)
            project(0, 0, 0, 0, range(1, 2), False)
            transpose_weights(MO)
            pe.wait_ge(wt_even, 4)
            pe.wait_ge(wt_odd, 4)
            project(0, 0, 0, 0, range(2, 3), False)
            pe.wait_ge(hT_ready, 4)
            pe.wait_ge(wmod_ga_loaded, 16)
            modulation(gT_ps[:, 0], wmod_ga, 0)
            pe.wait_ge(wmod2_loaded, 16)
            modulation(mod2_ps[:, SCALE2 - 2], wmod2, 1)
            modulation(mod2_ps[:, SHIFT2 - 2], wmod2, 0)
            pe.wait_ge(wmod_gb_loaded, 16)
            modulation(gT_ps[:, 1], wmod_gb, 0).then_inc(mod2_in_psum, 1)
            pe.wait_ge(g_step, 5)
            pe.wait_ge(mod2_ready, 2)
            for g in range(2):
                for c in range(CT):
                    last = nc.tensor.transpose(misc[0:B, 1 - g, c * P:(c + 1) * P], g_work[:, 5, g, c, :],
                                               per["ident"][:])
            last.then_inc(gate_rows_in_psum, 1)
            pe.wait_ge(gate_rows_ready, 2)

            def batch(b, first, last):
                for h in range(2):
                    s = b * 2 + h
                    u = b * 4 + 2 * h
                    ahead = not (last and h == 1)
                    if ahead:
                        if first:
                            pe.wait_ge(hT_ready, s * 4 + 4)
                        transposes(s + 1, 1 - h, range(0, 2), not first)
                    project(s, h, 1, u + 1, range(0, 1), True)
                    if ahead:
                        transposes(s + 1, 1 - h, range(2, 4), not first)
                    project(s, h, 1, u + 1, range(1, 3), True)
                    behind = not (first and h == 0)
                    if behind:
                        out_project(s - 1, 1 - h, range(0, 2), ahead)
                    if ahead:
                        project(s + 1, 1 - h, 0, u + 2, range(0, 1), True)
                    if behind:
                        out_project(s - 1, 1 - h, range(2, 4), ahead)
                    if ahead:
                        project(s + 1, 1 - h, 0, u + 2, range(1, 3), True)
            over_batches(pe, batch)
            out_project(STEPS - 1, 1, range(TT_), False)

        @block.vector
        def _(dve):
            def stats(s, h, x_count):
                if not isinstance(s, int) or s:
                    dve.wait_ge(lnv_ready, s)
                dve.wait_ge(x_loaded[h], x_count)
                for t in range(TT_):
                    nc.vector.bn_stats(bn6[:, t], xin[:, h, t]).then_inc(bn_ready, 1)

            def aggregate():
                for t in range(TT_):
                    nc.vector.bn_aggr(mv[:, t], bn6[:, t]).then_inc(mv_ready, 1)

            def neg_mean_rstd(s):
                if not isinstance(s, int) or s:
                    dve.wait_ge(xn_ready, s * 4)
                dve.wait_ge(mv_ready, s * 4 + 4)
                dve.wait_ge(rstd_ready, s + 1)
                nc.vector.scalar_tensor_tensor(out=nmr[:], in0=mv[:, :, 0], scalar=-1.0, in1=rstd[:],
                                               op0=ALU.mult, op1=ALU.mult).then_inc(nmr_ready, 1)

            def shift(s, h, first_step):
                if not first_step:
                    dve.wait_ge(mixsum_ready, s * 12)
                if h == 0:
                    nc.vector.memset(hT[:, :, 0], 0.0).then_inc(shift_ready, 1)
                else:
                    dve.wait_ge(hT_ready, s * 4)
                    nc.vector.tensor_copy(hT[:, :, 0], hT[:, :, ST]).then_inc(shift_ready, 1)

            def batch_mod(b, wait_free):
                if wait_free:
                    dve.wait_ge(hT_ready, b * 8)
                nc.vector.tensor_copy(mod[:], per["modT"][:, bass.ds(b, 1), 0:2, :].rearrange("p o q c -> p (o q) c")
                                      ).then_inc(mod_ready, 1)

            def add_shifted(s, m, cs):
                for c in cs:
                    if m == 0 and c == 0:
                        dve.wait_ge(shift_ready, s + 1)
                    dve.wait_ge(mixprod_ready, s * 12 + 4 * m + c + 1)
                    nc.vector.scalar_tensor_tensor(out=mix[m][:, c], in0=hT[:, c, 0:ST],
                                                   scalar=per["one_less_mix"][:, m, c:c + 1], in1=mix[m][:, c],
                                                   op0=ALU.mult, op1=ALU.add).then_inc(mixsum_ready, 1)

            def mix_rest(s, m):
                for k in range(0, CT, 2):
                    dve.wait_ge(mixhi_ready, s * 2 * SPLIT + 2 * m + k // 2 + 1)
                    nc.vector.tensor_tensor(mix_lo[:, m, k:k + 2], mix[m][:, k:k + 2], mix_hi[:, m, k:k + 2],
                                            ALU.subtract).then_inc(mixlo_ready, 1)

            def running_max(u, p, h):
                st = state[:, p]
                if h == 0:
                    nc.vector.memset(st[:, 0, :, 0], NEG_HUGE).then_inc(init_ready, 1)
                    nc.vector.memset(st[:, 1:3, :, 0], 0.0).then_inc(init_ready, 1)
                else:
                    nc.vector.tensor_copy(st[:, 0, :, 0], st[:, 0, :, ST]).then_inc(init_ready, 1)
                    nc.vector.tensor_copy(st[:, 1:3, :, 0], st[:, 1:3, :, ST]).then_inc(init_ready, 1)
                dve.wait_ge(k_ready, u + 1)
                dve.wait_ge(init_ready, u * 2 + 2)
                for i in range(2):
                    c = 2 * p + i
                    nc.vector.tensor_tensor_scan(st[:, 0, i, 1:ST + 1], per["w"][:, c:c + 1].to_broadcast([P, ST]),
                                                 kb[:, i], st[:, 0, i, 0:1], ALU.add, ALU.max
                                                 ).then_inc(max_ready, 1)
                dve.wait_ge(max_ready, u * 2 + 2)
                nc.vector.tensor_tensor(kp[:], kb[:], st[:, 0, :, 0:ST], ALU.subtract).then_inc(kp_ready, 1)

            def denominator_states(u, p):
                st = state[:, p]
                dve.wait_ge(ha_ready, u + 1)
                dve.wait_ge(e1_ready, u + 1)
                for i in range(2):
                    nc.vector.tensor_tensor_scan(st[:, 2, i, 1:ST + 1], e1[:, i], ha[:, i], st[:, 2, i, 0:1],
                                                 ALU.mult, ALU.add).then_inc(den_state, 1)

            def numerator_states(u, p, q):
                st = state[:, p]
                dve.wait_ge(v_ready, u + 1)
                dve.wait_ge(den_state, u * 2 + 2)
                nc.vector.tensor_tensor(ha[:], ha[:], vb[:, q], ALU.mult).then_inc(e2v_ready, 1)
                dve.wait_ge(e2v_ready, u + 1)
                for i in range(2):
                    nc.vector.tensor_tensor_scan(st[:, 1, i, 1:ST + 1], e1[:, i], ha[:, i], st[:, 1, i, 0:1],
                                                 ALU.mult, ALU.add).then_inc(num_state, 1)

            def outputs(u, p, q):
                st = state[:, p]
                dve.wait_ge(e2v_ready, u + 1)
                dve.wait_ge(ga_ready, u + 1)
                nc.vector.tensor_tensor(vb[:, q], ga[:], vb[:, q], ALU.mult).then_inc(n2_ready, 1)
                dve.wait_ge(gb_ready, u + 1)
                dve.wait_ge(num_state, u * 2 + 2)
                nc.vector.tensor_tensor(e1[:], gb[:], st[:, 1, :, 0:ST], ALU.mult).then_inc(n1_ready, 1)
                dve.wait_ge(n1_ready, u + 1)
                nc.vector.tensor_tensor(gb[:], gb[:], st[:, 2, :, 0:ST], ALU.mult).then_inc(d1_ready, 1)
                dve.wait_ge(n2_ready, u + 1)
                dve.wait_ge(d1_ready, u + 1)
                nc.vector.tensor_tensor(ga[:], ga[:], gb[:], ALU.add).then_inc(den_ready, 1)
                dve.wait_ge(eb_ready, u + 1)
                dve.wait_ge(den_ready, u + 1)
                nc.vector.scalar_tensor_tensor(out=ga[:], in0=eb[:, q], scalar=1.0, in1=ga[:], op0=ALU.add,
                                               op1=ALU.mult).then_inc(full_den_ready, 1)
                nc.vector.tensor_tensor(vb[:, q], vb[:, q], e1[:], ALU.add).then_inc(num_ready, 1)

            def log_plus_m(u, q):
                dve.wait_ge(log_ready, u + 1)
                dve.wait_ge(m_ready, u + 1)
                nc.vector.tensor_tensor(ga[:], ga[:], mb[:, q], ALU.add).then_inc(logm_ready, 1)

            def output(u, p, q, h, s, wait_free):
                if wait_free:
                    dve.wait_ge(o_in_psum, s * 4 - 4)
                dve.wait_ge(num_ready, u + 1)
                dve.wait_ge(inv_ready, u + 1)
                nc.vector.tensor_tensor(yT[:, h, 2 * p:2 * p + 2], vb[:, q], ga[:], ALU.mult).then_inc(y_ready, 1)

            def residual(step, b, ts):
                for t in ts:
                    if t == 0:
                        dve.wait_ge(gate_loaded, b * 16 + 16)
                    dve.wait_ge(o_in_psum, step * 4 + t + 1)
                    nc.vector.tensor_tensor(misc[:, t % 2], misc[:, t % 2], gate[:], ALU.mult).then_inc(gated_ready, 1)
                    dve.wait_ge(gated_ready, step * 4 + t + 1)
                    dve.wait_ge(xres_loaded, step * 16 + 16)
                    nc.vector.tensor_tensor(xres[:, t], misc[:, t % 2], xres[:, t], ALU.add).then_inc(res_ready, 1)

            def transposed_weights(m):
                if m < SPLIT:
                    for c in range(CT):
                        dve.wait_ge(wt_hi_ready, 4 * m + c + 1)
                        nc.vector.tensor_tensor(per["wT_lo"][:, m, c, :], proj[2][:, c % 2], per["wT_hi"][:, m, c, :],
                                                ALU.subtract).then_inc(wt_lo_ready, 1)
                else:
                    for c in range(1, CT, 2):
                        dve.wait_ge(wt_in_psum, 4 * m + c + 1)
                        nc.vector.tensor_copy(per["wT"][:, m - SPLIT, c, :], proj[2][:, 1]).then_inc(wt_odd, 1)

            def modulation_rows(ps, first_row, done):
                for q in range(2):
                    nc.vector.tensor_scalar(per["modT"][:, :, first_row + q, :].rearrange("p b c -> p c b"), ps[:, q],
                                            1.0 - q, None, ALU.add).then_inc(done, 1)

            dve.wait_ge(chan_in_psum, 1)
            nc.vector.tensor_copy(per["chan"][:].rearrange("p i c -> p (i c)"), chan_ps).then_inc(chan_ready, 1)
            dve.wait_ge(c_exp_ready, 1)
            nc.vector.tensor_scalar(silu_den[:], silu_exp[:], 1.0, None, ALU.add).then_inc(silu_step, 1)
            dve.wait_ge(silu_step, 1)
            nc.vector.reciprocal(silu_rec[:], silu_den[:]).then_inc(silu_step, 1)
            dve.wait_ge(silu_step, 2)
            nc.vector.tensor_tensor(siluT[:], cT_ps, silu_rec[:], ALU.mult).then_inc(silu_step, 1)
            dve.wait_ge(chan_ready, 1)
            nc.vector.tensor_scalar(per["one_less_mix"][:], per["chan"][:, 0:3, :], -1.0, 1.0, ALU.mult, ALU.add
                                    ).then_inc(const_ready, 1)
            nc.vector.tensor_scalar(per["neg_u"][:], per["chan"][:, 4, :], -1.0, None, ALU.mult
                                    ).then_inc(const_ready, 1)
            dve.wait_ge(decay_ready, 1)
            nc.vector.tensor_scalar(per["w"][:], per["neg_w"][:], -1.0, None, ALU.mult).then_inc(const_ready, 1)
            stats(0, 0, 16)
            dve.wait_ge(bn_ready, 4)
            shift(0, 0, True)
            aggregate()
            neg_mean_rstd(0)
            dve.wait_ge(mod1_in_psum, 1)
            modulation_rows(mod1_ps, SCALE1, mod1_ready)
            dve.wait_ge(mod1_ready, 2)
            batch_mod(0, False)
            dve.wait_ge(const_ready, 3)
            add_shifted(0, 0, range(CT))
            transposed_weights(0)
            mix_rest(0, 0)
            add_shifted(0, 1, range(CT))
            transposed_weights(1)
            mix_rest(0, 1)
            transposed_weights(2)
            add_shifted(0, 2, range(CT))
            transposed_weights(3)
            stats(1, 1, 16)
            dve.wait_ge(bn_ready, 8)
            aggregate()
            neg_mean_rstd(1)
            running_max(0, 0, 0)
            dve.wait_ge(mod2_in_psum, 1)
            g = [g_work[:, i] for i in range(6)]
            modulation_rows(mod2_ps, SCALE2, mod2_ready)
            nc.vector.tensor_copy(g[0], gT_ps).then_inc(g_step, 1)
            dve.wait_ge(g_step, 1)
            nc.vector.tensor_scalar(g[1], g[0], -1.0, None, ALU.mult).then_inc(g_step, 1)
            nc.vector.tensor_scalar(g[2], g[0], 0.0, 2.0, ALU.is_ge, ALU.mult).then_inc(g_step, 1)
            dve.wait_ge(g_step, 3)
            nc.vector.tensor_tensor(g[3], g[0], g[1], ALU.max).then_inc(g_step, 1)
            dve.wait_ge(g_step, 4)
            nc.vector.tensor_scalar(g[4], g[3], GATE_FLOOR, None, ALU.max).then_inc(g_floor, 1)
            dve.wait_ge(g_floor, 1)
            nc.vector.scalar_tensor_tensor(out=g[5], in0=g[2], scalar=1.0, in1=g[4], op0=ALU.subtract, op1=ALU.mult
                                           ).then_inc(g_step, 1)
            dve.wait_ge(gate_rows_in_psum, 1)
            for i in range(2):
                nc.vector.tensor_copy(gate_rows[:, i], misc[0:B, 1 - i, :]).then_inc(gate_rows_ready, 1)

            def batch(b, first, last):
                for h in range(2):
                    s = b * 2 + h
                    u = b * 4 + 2 * h
                    ahead = not (last and h == 1)
                    behind = not (first and h == 0)
                    if ahead:
                        if h == 1:
                            batch_mod(b + 1, True)
                        shift(s + 1, 1 - h, False)
                    denominator_states(u, 0)
                    numerator_states(u, 0, 0)
                    outputs(u, 0, 0)
                    log_plus_m(u, 0)
                    running_max(u + 1, 1, h)
                    if ahead:
                        add_shifted(s + 1, 0, range(0, 2))
                    output(u, 0, 0, h, s, not first)
                    if ahead:
                        add_shifted(s + 1, 0, range(2, 4))
                    if not last:
                        stats(s + 2, h, b * 16 + 32)
                        dve.wait_ge(bn_ready, s * 4 + 12)
                    denominator_states(u + 1, 1)
                    if not last:
                        aggregate()
                    if ahead:
                        mix_rest(s + 1, 0)
                    numerator_states(u + 1, 1, 1)
                    if ahead:
                        add_shifted(s + 1, 1, range(CT))
                    if behind:
                        residual(s - 1, b - 1 + h, range(0, 2))
                    if ahead:
                        mix_rest(s + 1, 1)
                    if not last:
                        neg_mean_rstd(s + 2)
                    outputs(u + 1, 1, 1)
                    if ahead:
                        add_shifted(s + 1, 2, range(CT))
                    log_plus_m(u + 1, 1)
                    if ahead:
                        running_max(u + 2, 0, 1 - h)
                    output(u + 1, 1, 1, h, s, not first)
                    if behind:
                        residual(s - 1, b - 1 + h, range(2, 4))
            over_batches(dve, batch)
            residual(STEPS - 1, B - 1, range(TT_))


def ffn(nc, io, per, out):
    with ExitStack() as ctx:
        def sb(name, shape, dt=F32):
            return ctx.enter_context(nc.sbuf_tensor(name, shape, dt))

        def sem(name):
            return ctx.enter_context(nc.semaphore(name))

        xT_hi = sb("xT_hi", [P, CT, NTOK], F32R)
        xT_lo = sb("xT_lo", [P, CT, NTOK], F32R)
        w1_hi = sb("w1_hi", [P, 2, CT, FT * P], F32R)
        w1_lo = sb("w1_lo", [P, 2, CT, FT * P], F32R)
        w2_hi = sb("w2_hi", [P, 2, FT, C], F32R)
        w2_lo = sb("w2_lo", [P, 2, FT, C], F32R)
        wraw = sb("ffn_wraw", [P, CT, C])
        y = sb("y", [P, TOKT, C])
        h_raw = sb("h_raw", [P, 2, ST])
        h_hi = sb("h_hi", [P, 2, FT, ST], F32R)
        h_lo = sb("h_lo", [P, 2, FT, ST], F32R)
        bn6 = sb("ffn_bn6", [P, TOKT, 6])
        mv = sb("ffn_mv", [P, TOKT, 2])
        lnv = sb("ffn_lnv", [P, TOKT])
        rstd = sb("ffn_rstd", [P, TOKT])
        nmr = sb("ffn_nmr", [P, TOKT])
        ew = sb("ew", [P, TOKT, 2])
        wsum = sb("wsum", [P, TOKT])
        gate, x1 = wraw[:, 0:2], wraw[:, 2:4]
        up = ctx.enter_context(nc.psum_tensor("up", [P, FT, ST], F32))
        down = ctx.enter_context(nc.psum_tensor("down", [P, TT_, C], F32))

        x_loaded = [sem(f"ffn_x_loaded{c}") for c in range(CHUNKS)]
        ew_loaded = sem("ew_loaded")
        gates_loaded = sem("gates_loaded")
        wraw_loaded = [sem("w1_loaded"), sem("w2_loaded")]
        bn_ready = sem("ffn_bn_ready")
        mv_ready = sem("ffn_mv_ready")
        lnv_ready = sem("ffn_lnv_ready")
        rstd_ready = sem("ffn_rstd_ready")
        nmr_ready = sem("ffn_nmr_ready")
        xn_ready = sem("ffn_xn_ready")
        xnT_in_psum = sem("ffn_xnT_in_psum")
        xT_ready = sem("ffn_xT_ready")
        xhi_ready = sem("xhi_ready")
        xlo_ready = sem("xlo_ready")
        wsum_ready = sem("wsum_ready")
        zero_ready = sem("y_zeroed")
        whi_ready = [sem("w1_hi_ready"), sem("w2_hi_ready")]
        wlo_ready = [sem("w1_lo_ready"), sem("w2_lo_ready")]
        h_in_psum = sem("h_in_psum")
        gelu_ready = sem("gelu_ready")
        hhi_ready = sem("hhi_ready")
        hlo_ready = sem("hlo_ready")
        y_in_psum = sem("y_in_psum")
        y_ready = sem("ffn_y_ready")
        x1_loaded = [sem("x1_loaded0"), sem("x1_loaded1")]
        scaled_ready = sem("scaled_ready")
        sum_ready = sem("sum_ready")
        final_stored = [sem("final_stored0"), sem("final_stored1")]

        rows = out[0:NTOK, :].rearrange("(n p) c -> p n c", p=P)
        w_rows = [io["w1"].rearrange("(c p) (g n) -> g p c n", p=P, n=FT * P),
                  io["w2"].rearrange("(g f p) n -> g p f n", f=FT, p=P)]
        w_hi, w_lo = (w1_hi, w2_hi), (w1_lo, w2_lo)
        block = ctx.enter_context(nc.Block())
        JOBS = 2 * CHUNKS
        TURNS = GROUPS // 2

        def over_turns(eng, turn):
            turn(0, True, False)
            with eng.Fori(1, TURNS - 1) as it:
                turn(it, False, False)
            turn(TURNS - 1, False, True)

        @block.sync
        def _(sp):
            sp.dma_start(y[:, 0:4], rows[:, 0:4]).then_inc(x_loaded[0], 16)
            sp.dma_start(wraw[:], w_rows[0][0]).then_inc(wraw_loaded[0], 16)
            for c in range(1, CHUNKS):
                sp.dma_start(y[:, 4 * c:4 * c + 4], rows[:, 4 * c:4 * c + 4]).then_inc(x_loaded[c], 16)
            sp.wait_ge(wlo_ready[0], 2)
            sp.dma_start(wraw[:], w_rows[1][0]).then_inc(wraw_loaded[1], 16)
            sp.dma_start(ew[:], io["ew"].rearrange("(n p) k -> p n k", p=P)).then_inc(ew_loaded, 16)
            with sp.Fori(1, GROUPS) as g:
                for i in range(2):
                    if i == 0:
                        sp.wait_ge(wlo_ready[1], g * 2)
                    else:
                        sp.wait_ge(wlo_ready[0], g * 2 + 2)
                    sp.dma_start(wraw[:], w_rows[i][bass.ds(g, 1)].rearrange("o p c n -> (o p) c n")
                                 ).then_inc(wraw_loaded[i], 16)
            sp.wait_ge(wlo_ready[1], GROUPS * 2)
            for b in range(2):
                sp.dma_start(gate[:, b], per["gates"][1, b:b + 1, :].to_broadcast([P, C])).then_inc(gates_loaded, 16)
            for n in range(TOKT + 1):
                if n < TOKT:
                    if n >= 2:
                        sp.wait_ge(final_stored[n % 2], n // 2 * 16)
                    sp.dma_start(x1[:, n % 2], rows[:, n]).then_inc(x1_loaded[n % 2], 16)
                if n >= 1:
                    sp.wait_ge(sum_ready, n)
                    sp.dma_start(rows[:, n - 1], x1[:, (n - 1) % 2]).then_inc(final_stored[(n - 1) % 2], 16)
            for i in range(2):
                sp.wait_ge(final_stored[i], TOKT // 2 * 16)

        @block.scalar
        def _(act):
            def split_weights(g, q, i):
                act.wait_ge(wraw_loaded[i], g * 16 + 16)
                for k in range(2):
                    nc.scalar.activation(w_hi[i][:, q, 2 * k:2 * k + 2], wraw[:, 2 * k:2 * k + 2], ACT.Copy
                                         ).then_inc(whi_ready[i], 1)

            def gelu(job, q, raw_used, half_used):
                for f in range(FT):
                    act.wait_ge(h_in_psum, job * 4 + f + 1)
                    if raw_used or f >= 2:
                        act.wait_ge(hlo_ready, job * 4 - 1 + f)
                    nc.scalar.activation(h_raw[:, f % 2], up[:, f], ACT.Gelu_apprx_tanh).then_inc(gelu_ready, 1)
                    act.wait_ge(gelu_ready, job * 4 + f + 1)
                    if f == 0 and half_used:
                        act.wait_ge(y_in_psum, job * 4 - 4)
                    nc.scalar.activation(h_hi[:, q, f], h_raw[:, f % 2], ACT.Copy).then_inc(hhi_ready, 1)

            def chunk_rstd(c):
                ts = slice(4 * c, 4 * c + 4)
                act.wait_ge(mv_ready, 4 * c + 4)
                nc.scalar.activation(lnv[:, ts], mv[:, ts, 1], ACT.Ln, bias=per["eps"][:, 0:1]).then_inc(lnv_ready, 1)
                act.wait_ge(lnv_ready, c + 1)
                nc.scalar.activation(rstd[:, ts], lnv[:, ts], ACT.Exp, scale=-0.5).then_inc(rstd_ready, 1)

            def chunk_normalise(c):
                act.wait_ge(nmr_ready, c + 1)
                for t in range(4 * c, 4 * c + 4):
                    nc.scalar.activation(y[:, t], y[:, t], ACT.Identity, bias=nmr[:, t:t + 1], scale=rstd[:, t:t + 1]
                                         ).then_inc(xn_ready, 1)

            def chunk_modulate(c):
                for k in range(CT):
                    act.wait_ge(xnT_in_psum, 4 * c + k + 1)
                    if c == 1 and k < 2:
                        act.wait_ge(hlo_ready, 4)
                    elif 4 * c + k >= 2:
                        act.wait_ge(xlo_ready, 4 * c + k - 1)
                    b = c // 2
                    nc.scalar.activation(h_raw[:, k % 2], down[:, k], ACT.Identity,
                                         bias=per["modT"][:, b, SHIFT2, k:k + 1],
                                         scale=per["modT"][:, b, SCALE2, k:k + 1]).then_inc(xT_ready, 1)
                    act.wait_ge(xT_ready, 4 * c + k + 1)
                    nc.scalar.activation(xT_hi[:, k, c * ST:(c + 1) * ST], h_raw[:, k % 2], ACT.Copy
                                         ).then_inc(xhi_ready, 1)

            chunk_rstd(0)
            chunk_normalise(0)
            split_weights(0, 0, 0)
            chunk_modulate(0)
            for c in range(1, CHUNKS):
                chunk_rstd(c)
                chunk_normalise(c)
            act.wait_ge(xlo_ready, 4)
            gelu(0, 0, False, False)
            chunk_modulate(1)
            split_weights(0, 0, 1)
            chunk_modulate(2)
            chunk_modulate(3)
            act.wait_ge(xlo_ready, 4 * CHUNKS)

            def turn(it, first, last):
                for j in range(JOBS):
                    job = it * JOBS + j
                    if not (last and j == JOBS - 1):
                        gelu(job + 1, (j + 1) % 2, True, not (first and j == 0))
                    if j % CHUNKS in (1, 2) and not (last and j > CHUNKS):
                        g = it * 2 + j // CHUNKS
                        if j % CHUNKS == 1 and not (first and j == 1):
                            act.wait_ge(y_in_psum, g * 16)
                        split_weights(g + 1, (j // CHUNKS + 1) % 2, j % CHUNKS - 1)
            over_turns(act, turn)

        @block.gpsimd
        def _(pool):
            for c in range(CHUNKS):
                pool.wait_ge(xnT_in_psum, 4 * c + 4)
                pool.memset(y[:, 4 * c:4 * c + 4], 0.0).then_inc(zero_ready, 1)

        @block.tensor
        def _(pe):
            def first_product(job, g, q, chunk, prologue, group0):
                if group0:
                    pe.wait_ge(xlo_ready, 4 * chunk + 4)
                pe.wait_ge(wlo_ready[0], g * 2 + 2)
                for f in range(FT):
                    if not prologue:
                        pe.wait_ge(gelu_ready, job * 4 - 3 + f)
                    fs, ts = slice(f * P, (f + 1) * P), slice(chunk * ST, (chunk + 1) * ST)
                    for c in range(CT):
                        hi, lo = w1_hi[:, q, c, fs], w1_lo[:, q, c, fs]
                        nc.tensor.matmul(up[:, f], hi, xT_hi[:, c, ts], start=(c == 0), stop=False)
                        nc.tensor.matmul(up[:, f], hi, xT_lo[:, c, ts], start=False, stop=False)
                        last = nc.tensor.matmul(up[:, f], lo, xT_hi[:, c, ts], start=False, stop=(c == CT - 1))
                    last.then_inc(h_in_psum, 1)

            def second_product(job, g, q, hq, old):
                pe.wait_ge(hlo_ready, job * 4 + 4)
                pe.wait_ge(wlo_ready[1], g * 2 + 2)
                for t in range(TT_):
                    if old:
                        pe.wait_ge(y_ready, job * 4 - 3 + t)
                    else:
                        pe.wait_ge(xT_ready, 4 * CHUNKS)
                    ts = slice(t * P, (t + 1) * P)
                    for f in range(FT):
                        hi, lo = h_hi[:, hq, f, ts], h_lo[:, hq, f, ts]
                        nc.tensor.matmul(down[:, t], hi, w2_hi[:, q, f], start=(f == 0), stop=False)
                        nc.tensor.matmul(down[:, t], hi, w2_lo[:, q, f], start=False, stop=False)
                        last = nc.tensor.matmul(down[:, t], lo, w2_hi[:, q, f], start=False, stop=(f == FT - 1))
                    last.then_inc(y_in_psum, 1)

            def chunk_transposes(c):
                pe.wait_ge(xn_ready, 4 * c + 4)
                for k in range(CT):
                    if c >= 1:
                        pe.wait_ge(xT_ready, 4 * c - 3 + k)
                    for t in range(TT_):
                        last = nc.tensor.transpose(down[:, k, t * P:(t + 1) * P], y[:, 4 * c + t, k * P:(k + 1) * P],
                                                   per["ident"][:])
                    last.then_inc(xnT_in_psum, 1)

            chunk_transposes(0)
            first_product(0, 0, 0, 0, True, True)
            for c in range(1, CHUNKS):
                chunk_transposes(c)

            def turn(it, first, last):
                for j in range(JOBS):
                    job = it * JOBS + j
                    n = j + 1
                    if not (last and j == JOBS - 1):
                        first_product(job + 1, it * 2 + n // CHUNKS, (n // CHUNKS) % 2, n % CHUNKS, False,
                                      first and n < CHUNKS)
                    second_product(job, it * 2 + j // CHUNKS, j // CHUNKS, j % 2, not (first and j == 0))
            over_turns(pe, turn)

        @block.vector
        def _(dve):
            def split_rest(g, q, i):
                for k in range(2):
                    dve.wait_ge(whi_ready[i], g * 2 + k + 1)
                    nc.vector.tensor_tensor(w_lo[i][:, q, 2 * k:2 * k + 2], wraw[:, 2 * k:2 * k + 2],
                                            w_hi[i][:, q, 2 * k:2 * k + 2], ALU.subtract
                                            ).then_inc(wlo_ready[i], 1)

            def h_rest(job, q, half_used):
                for f in range(FT):
                    dve.wait_ge(hhi_ready, job * 4 + f + 1)
                    if f == 0 and half_used:
                        dve.wait_ge(y_in_psum, job * 4 - 4)
                    nc.vector.tensor_tensor(h_lo[:, q, f], h_raw[:, f % 2], h_hi[:, q, f], ALU.subtract
                                            ).then_inc(hlo_ready, 1)

            def accumulate(job, chunk, old):
                for t in range(TT_):
                    n = chunk * TT_ + t
                    dve.wait_ge(y_in_psum, job * 4 + t + 1)
                    if old:
                        dve.wait_ge(y_ready, job * 4 - 4 * CHUNKS + t + 1)
                    nc.vector.tensor_tensor(y[:, n], down[:, t], y[:, n], ALU.add).then_inc(y_ready, 1)

            def chunk_stats(c):
                ts = slice(4 * c, 4 * c + 4)
                dve.wait_ge(x_loaded[c], 16)
                for t in range(4 * c, 4 * c + 4):
                    nc.vector.bn_stats(bn6[:, t], y[:, t]).then_inc(bn_ready, 1)
                for t in range(4 * c, 4 * c + 4):
                    dve.wait_ge(bn_ready, t + 1)
                    nc.vector.bn_aggr(mv[:, t], bn6[:, t]).then_inc(mv_ready, 1)
                dve.wait_ge(mv_ready, 4 * c + 4)
                dve.wait_ge(rstd_ready, c + 1)
                nc.vector.scalar_tensor_tensor(out=nmr[:, ts], in0=mv[:, ts, 0], scalar=-1.0, in1=rstd[:, ts],
                                               op0=ALU.mult, op1=ALU.mult).then_inc(nmr_ready, 1)

            def chunk_rest(c):
                for k in range(CT):
                    dve.wait_ge(xhi_ready, 4 * c + k + 1)
                    cs = slice(c * ST, (c + 1) * ST)
                    nc.vector.tensor_tensor(xT_lo[:, k, cs], h_raw[:, k % 2], xT_hi[:, k, cs], ALU.subtract
                                            ).then_inc(xlo_ready, 1)

            chunk_stats(0)
            split_rest(0, 0, 0)
            chunk_rest(0)
            for c in range(1, CHUNKS):
                chunk_stats(c)
            h_rest(0, 0, False)
            chunk_rest(1)
            split_rest(0, 0, 1)
            chunk_rest(2)
            chunk_rest(3)
            dve.wait_ge(ew_loaded, 16)
            nc.vector.tensor_tensor(wsum[:], ew[:, :, 0], ew[:, :, 1], ALU.add).then_inc(wsum_ready, 1)
            dve.wait_ge(zero_ready, CHUNKS)

            def finish(chunk):
                if chunk == 0:
                    dve.wait_ge(gates_loaded, 32)
                    dve.wait_ge(wsum_ready, 1)
                for n in range(4 * chunk, 4 * chunk + 4):
                    dve.wait_ge(y_ready, (GROUPS - 1) * CHUNKS * 4 + n + 1)
                    nc.vector.scalar_tensor_tensor(out=y[:, n], in0=y[:, n], scalar=wsum[:, n:n + 1],
                                                   in1=gate[:, n // (T // P)], op0=ALU.mult, op1=ALU.mult
                                                   ).then_inc(scaled_ready, 1)
                for n in range(4 * chunk, 4 * chunk + 4):
                    dve.wait_ge(scaled_ready, n + 1)
                    dve.wait_ge(x1_loaded[n % 2], n // 2 * 16 + 16)
                    nc.vector.tensor_tensor(x1[:, n % 2], y[:, n], x1[:, n % 2], ALU.add).then_inc(sum_ready, 1)

            def turn(it, first, last):
                for j in range(JOBS):
                    job = it * JOBS + j
                    if not (last and j == JOBS - 1):
                        h_rest(job + 1, (j + 1) % 2, not (first and j == 0))
                    accumulate(job, j % CHUNKS, not (first and j < CHUNKS))
                    if last and j >= CHUNKS:
                        finish(j - CHUNKS)
                    if j % CHUNKS in (1, 2) and not (last and j > CHUNKS):
                        split_rest(it * 2 + j // CHUNKS + 1, (j // CHUNKS + 1) % 2, j % CHUNKS - 1)
            over_turns(dve, turn)


def adaln_rwkv_ffn(nc, io, out):
    with ExitStack() as ctx:
        def sb(name, shape, dt=F32):
            return ctx.enter_context(nc.sbuf_tensor(name, shape, dt))

        scratch = {"gates": nc.dram_tensor("gates", (2, B, C), F32, kind="Internal").ap()}
        per = {
            "ident": sb("ident", [P, P]),
            "eps": sb("eps", [P, 1]),
            "chan": sb("chan", [P, 5, CT]),
            "one_less_mix": sb("one_less_mix", [P, 3, CT]),
            "neg_w": sb("neg_w", [P, CT]),
            "w": sb("w", [P, CT]),
            "neg_u": sb("neg_u", [P, CT]),
            "modT": sb("modT", [P, B, 4, CT]),
            "gates": scratch["gates"],
        }
        with ExitStack() as attention_only:
            for name, count, dt in (("wT", 4 - SPLIT, F32), ("wT_hi", SPLIT, F32R), ("wT_lo", SPLIT, F32R)):
                per[name] = attention_only.enter_context(nc.sbuf_tensor(name, [P, count, CT, C], dt))
            attention(nc, io, per, scratch, out)
        ffn(nc, io, per, out)


_INS = {
    "L0_attn_x": "x", "L0_attn_time_decay": "decay", "L0_attn_time_first": "first", "L0_attn_time_mix_k": "mix_k",
    "L0_attn_time_mix_v": "mix_v", "L0_attn_time_mix_r": "mix_r", "L0_attn_Wk": "Wk", "L0_attn_Wv": "Wv",
    "L0_attn_Wr": "Wr", "L0_attn_Wo": "Wo", "L0_ffn_expert_weights": "ew", "L0_ffn_w1": "w1", "L0_ffn_w2": "w2",
    "L0_c": "c", "L0_wmod": "wmod",
}


def kernel(**inputs):
    import numpy as _np
    import concourse.bacc as _bacc
    from concourse import mybir as _mybir
    from concourse.bass_utils import run_bass_kernel_spmd as _run

    nc = _bacc.Bacc("TRN2", target_bir_lowering=False, num_devices=1, dynamic_dma_scratch_size=1024)
    arrays, io = {}, {}
    for name, short in _INS.items():
        a = _np.ascontiguousarray(inputs[name])
        if short == "x":
            a = a.reshape(B * T, C)
        if short.startswith("mix"):
            a = a.reshape(C)
        arrays[f"in_{short}"] = a
        io[short] = nc.dram_tensor(f"in_{short}", a.shape, _mybir.dt.from_np(a.dtype), kind="ExternalInput").ap()
    out = nc.dram_tensor("out_0", (B * T, C), _mybir.dt.float32, kind="ExternalOutput").ap()
    adaln_rwkv_ffn(nc, io, out)
    r = _run(nc, [arrays], core_ids=[0])
    return r.results[0]["out_0"].reshape(B, T, C)
```

```python
from contextlib import ExitStack

import concourse.bass as bass
from concourse import mybir

P = 128
F32 = mybir.dt.float32
F32R = mybir.dt.float32r
ALU = mybir.AluOpType
ACT = mybir.ActivationFunctionType

EPS = 1e-5
LN_EXP_SET = 6
NEG_HUGE = -1e38
GATE_FLOOR = 0.25

B, T, C = 8, 1024, 512
CT = C // P
ST = 512
TT_ = ST // P
STEPS = B * T // ST
NTOK = 2048
FT = 4
FH = 4096
GROUPS = FH // (FT * P)
CHUNKS = NTOK // ST
TOKT = NTOK // P
MK, MV, MR, MO = range(4)
SPLIT = 2
SCALE1, SHIFT1, SCALE2, SHIFT2 = range(4)


def attention(nc, io, per, scratch, out):
    with ExitStack() as ctx:
        def sb(name, shape, dt=F32):
            return ctx.enter_context(nc.sbuf_tensor(name, shape, dt))

        def sem(name):
            return ctx.enter_context(nc.semaphore(name))

        xin = sb("xin", [P, 2, TT_, C])
        xres = sb("xres", [P, TT_, C])
        gate = sb("gate", [P, C])
        bn6 = sb("bn6", [P, TT_, 6])
        mv = sb("mv", [P, TT_, 2])
        lnv = sb("lnv", [P, TT_])
        rstd = sb("rstd", [P, TT_])
        nmr = sb("nmr", [P, TT_])
        mod = sb("mod", [P, 2, CT])
        hT = sb("hT", [P, CT, ST + 1])
        mix_hi = sb("mix_hi", [P, SPLIT, CT, ST], F32R)
        mix_lo = sb("mix_lo", [P, SPLIT, CT, ST], F32R)
        whole = sb("whole", [P, 2, CT, ST])
        mix = [whole[:, 0], whole[:, 1], whole[:, 1]]
        state = sb("state", [P, 2, 3, 2, ST + 1])
        k_bufs = sb("k_bufs", [P, 2, 2, ST])
        kb, kp = k_bufs[:, 0], k_bufs[:, 1]
        vb = sb("vb", [P, 2, 2, ST])
        r_bufs = sb("r_bufs", [P, 2, 2, ST])
        mb, eb = r_bufs[:, 0], r_bufs[:, 1]
        wo_ga = sb("wo_ga", [P, CT, C])
        state_bufs = sb("state_bufs", [P, 2, 2, ST])
        e1, ha = state_bufs[:, 0], state_bufs[:, 1]
        out_weights = sb("out_weights", [P, 2, 2, ST])
        ga, gb = out_weights[:, 0], out_weights[:, 1]
        yT = sb("yT", [P, 2, CT, ST])
        proj = [ctx.enter_context(nc.psum_tensor(f"proj{m}", [P, 2, ST], F32)) for m in range(3)]
        misc = ctx.enter_context(nc.psum_tensor("misc", [P, 2, ST], F32))

        c_in = gate[0:B, :]
        chan_rows = state_bufs[0:5 * CT, 0, 0, 0:P]
        w_raw = [t[:].rearrange("p a b c -> p (a b) c") for t in (k_bufs, vb, r_bufs)] + [wo_ga[:]]
        wmod1 = whole[:].rearrange("p m c t -> p (m c t)").rearrange("p (k n) -> p k n", k=CT)
        wmod_ga = yT[:, 1]
        wmod_gb = xres
        mod_rows = ha[0:B, 0:2, :]
        gate_rows, gate_abs = wo_ga[0:B, 0:2, :], wo_ga[0:B, 2:4, :]
        pair1 = state[:, 1].rearrange("p a i t -> p (a i t)")
        silu_exp, silu_den, silu_rec = (
            pair1[:, i * CT * B:(i + 1) * CT * B].rearrange("p (c b) -> p c b", c=CT) for i in range(3))
        siluT = per["siluT"]
        chan_ps = misc[:, 0, 0:5 * CT]
        cT_ps = misc[:, 1, 0:CT * B].rearrange("p (k b) -> p k b", k=CT)
        wmod2 = xin[:].rearrange("p h t c -> p (h t) c").rearrange("p (k q) c -> p k q c", k=CT)
        mod2_rows = whole[0:B, 0, 0:2, :]
        mod2_ps = proj[1][:, 1, 0:2 * CT * B].rearrange("p (q c b) -> p q c b", q=2, c=CT)
        mod1_ps = proj[1][:, 0, 0:2 * CT * B].rearrange("p (q c b) -> p q c b", q=2, c=CT)

        c_loaded = sem("c_loaded")
        chan_loaded = sem("chan_loaded")
        w_loaded = [sem(f"w_loaded{m}") for m in range(4)]
        wmod1_loaded = sem("wmod1_loaded")
        wmod_ga_loaded = sem("wmod_ga_loaded")
        wmod_gb_loaded = sem("wmod_gb_loaded")
        ident_zero = sem("ident_zero")
        ident_ready = sem("ident_ready")
        eps_ready = sem("eps_ready")
        chan_in_psum = sem("chan_in_psum")
        chan_ready = sem("chan_ready")
        const_ready = sem("const_ready")
        decay_ready = sem("decay_ready")
        cT_in_psum = sem("cT_in_psum")
        c_exp_ready = sem("c_exp_ready")
        silu_step = sem("silu_step")
        mod_rows_in_psum = sem("mod_rows_in_psum")
        mod_rows_ready = sem("mod_rows_ready")
        mod1_in_psum = sem("mod1_in_psum")
        mod1_ready = sem("mod1_ready")
        gates_in_psum = sem("gates_in_psum")
        gates_taken = sem("gates_taken")
        gate_rows_ready = sem("gate_rows_ready")
        gates_stored = sem("gates_stored")
        wmod2_loaded = sem("wmod2_loaded")
        mod2_rows_in_psum = sem("mod2_rows_in_psum")
        mod2_rows_ready = sem("mod2_rows_ready")
        mod2_in_psum = sem("mod2_in_psum")
        mod2_ready = sem("mod2_ready")
        wt_in_psum = sem("wt_in_psum")
        wt_hi_ready = sem("wt_hi_ready")
        wt_lo_ready = sem("wt_lo_ready")
        wt_even = sem("wt_even")
        wt_odd = sem("wt_odd")

        x_loaded = [sem("x_loaded0"), sem("x_loaded1")]
        xres_loaded = sem("xres_loaded")
        gate_loaded = sem("gate_loaded")
        out_stored = sem("out_stored")
        mod_ready = sem("mod_ready")
        bn_ready = sem("bn_ready")
        mv_ready = sem("mv_ready")
        lnv_ready = sem("lnv_ready")
        rstd_ready = sem("rstd_ready")
        nmr_ready = sem("nmr_ready")
        xn_ready = sem("xn_ready")
        xnT_in_psum = sem("xnT_in_psum")
        shift_ready = sem("shift_ready")
        hT_ready = sem("hT_ready")
        mixprod_ready = sem("mixprod_ready")
        mixsum_ready = sem("mixsum_ready")
        mixhi_ready = sem("mixhi_ready")
        mixlo_ready = sem("mixlo_ready")
        in_psum = [sem("k_in_psum"), sem("v_in_psum"), sem("r_in_psum")]
        k_ready = sem("k_ready")
        v_ready = sem("v_ready")
        m_ready = sem("m_ready")
        absr_ready = sem("absr_ready")
        eb_ready = sem("eb_ready")
        init_ready = sem("init_ready")
        max_ready = sem("max_ready")
        kp_ready = sem("kp_ready")
        e1_arg = sem("e1_arg")
        ha_arg = sem("ha_arg")
        ga_arg = sem("ga_arg")
        gb_arg = sem("gb_arg")
        e1_ready = sem("e1_ready")
        ha_ready = sem("ha_ready")
        ga_ready = sem("ga_ready")
        gb_ready = sem("gb_ready")
        den_state = sem("den_state")
        e2v_ready = sem("e2v_ready")
        num_state = sem("num_state")
        n2_ready = sem("n2_ready")
        state_out = sem("state_out")
        den_ready = sem("den_ready")
        full_den_ready = sem("full_den_ready")
        log_ready = sem("log_ready")
        logm_ready = sem("logm_ready")
        inv_ready = sem("inv_ready")
        num_ready = sem("num_ready")
        y_ready = sem("y_ready")
        o_in_psum = sem("o_in_psum")
        wo_ready = sem("wo_ready")
        res_ready = sem("res_ready")

        x_rows = io["x"].rearrange("(s t p) c -> s p t c", t=TT_, p=P)
        out_rows = out.rearrange("(s t p) c -> s p t c", t=TT_, p=P)
        block = ctx.enter_context(nc.Block())

        def over_batches(eng, batch):
            batch(0, first=True, last=False)
            with eng.Fori(1, B - 1) as b:
                batch(b, first=False, last=False)
            batch(B - 1, first=False, last=True)

        @block.sync
        def _(sp):
            def load_x(b, h):
                s = b * 2 + h
                sp.dma_start(xin[:, h], x_rows[bass.ds(s, 1)].rearrange("o p t c -> (o p) t c")
                             ).then_inc(x_loaded[h], 16)

            def load_gate(b):
                sp.dma_start(gate[:], scratch["gates"][0, bass.ds(b, 1), :].to_broadcast([P, C])
                             ).then_inc(gate_loaded, 16)

            def residual(step, wait_stored):
                if wait_stored:
                    sp.wait_ge(out_stored, step * 16)
                sp.dma_start(xres[:], x_rows[bass.ds(step, 1)].rearrange("o p t c -> (o p) t c")
                             ).then_inc(xres_loaded, 16)
                sp.wait_ge(res_ready, step * 4 + 4)
                sp.dma_start(out_rows[bass.ds(step, 1)].rearrange("o p t c -> (o p) t c"), xres[:]
                             ).then_inc(out_stored, 16)

            sp.dma_start(c_in, io["c"]).then_inc(c_loaded, 16)
            for i, name in enumerate(("mix_k", "mix_v", "mix_r", "decay", "first")):
                sp.dma_start(chan_rows[i * CT:(i + 1) * CT, :], io[name].rearrange("(c p) -> c p", p=P)
                             ).then_inc(chan_loaded, 16)
            wmod_rows = io["wmod"].rearrange("(k p) n -> p k n", p=P)
            for m, name in enumerate(("Wk", "Wv", "Wr", "Wo")):
                if m == 2:
                    load_x(0, 0)
                    sp.dma_start(wmod1, wmod_rows[:, :, 0:2 * C]).then_inc(wmod1_loaded, 16)
                sp.dma_start(w_raw[m], io[name].rearrange("(t p) c -> p t c", p=P)).then_inc(w_loaded[m], 16)
            load_x(0, 1)
            sp.dma_start(wmod_ga, wmod_rows[:, :, 2 * C:3 * C]).then_inc(wmod_ga_loaded, 16)
            sp.dma_start(wmod_gb[:], wmod_rows[:, :, 5 * C:6 * C]).then_inc(wmod_gb_loaded, 16)
            sp.wait_ge(xnT_in_psum, 4)
            load_x(1, 0)

            def batch(b, first, left):
                for h in range(2):
                    s = b * 2 + h
                    if first and h == 1:
                        sp.wait_ge(gate_rows_ready, 1)
                        sp.dma_start(scratch["gates"].rearrange("g b c -> b g c"), gate_rows).then_inc(gates_stored, 16)
                        sp.wait_ge(gates_stored, 16)
                        load_gate(b)
                    if not first and h == 0:
                        sp.wait_ge(wo_ready, b * 4)
                        load_gate(b)
                    if left > h:
                        sp.wait_ge(xnT_in_psum, s * 4 + 8)
                        load_x(b + 1 + h, 1 - h)
                    if left == 0 and h == 0:
                        sp.wait_ge(xnT_in_psum, STEPS * 4)
                        sp.dma_start(wmod2.rearrange("p k q c -> p k (q c)"), wmod_rows[:, :, 3 * C:5 * C]
                                     ).then_inc(wmod2_loaded, 16)
                    if not (first and h == 0):
                        residual(s - 1, not first)

            batch(0, True, 2)
            with sp.Fori(1, B - 2) as b:
                batch(b, False, 2)
            batch(B - 2, False, 1)
            batch(B - 1, False, 0)
            step = STEPS - 1
            sp.wait_ge(out_stored, step * 16)
            sp.dma_start(xres[:], x_rows[step]).then_inc(xres_loaded, 16)
            for t in range(TT_):
                sp.wait_ge(res_ready, step * 4 + t + 1)
                sp.dma_start(out_rows[step, :, t], xres[:, t]).then_inc(out_stored, 16)
            sp.wait_ge(out_stored, (step + TT_) * 16)

        @block.gpsimd
        def _(pool):
            pool.memset(per["ident"][:], 0.0).then_inc(ident_zero, 1)
            pool.memset(per["eps"][:], EPS).then_inc(eps_ready, 1)
            pool.wait_ge(ident_zero, 1)
            pool.affine_select(out=per["ident"][:], in_=per["ident"][:], compare_op=ALU.not_equal, fill=1.0, base=0,
                               pattern=[[-1, P]], channel_multiplier=1).then_inc(ident_ready, 1)

        @block.scalar
        def _(act):
            def transposed_weights(m):
                for c in range(0, CT, 1 if m < SPLIT else 2):
                    act.wait_ge(wt_in_psum, 4 * m + c + 1)
                    if m < SPLIT:
                        nc.scalar.activation(per["wT_hi"][:, m, c, :], proj[2][:, c % 2], ACT.Copy
                                             ).then_inc(wt_hi_ready, 1)
                    else:
                        nc.scalar.activation(per["wT"][:, m - SPLIT, c, :], proj[2][:, 0], ACT.Copy
                                             ).then_inc(wt_even, 1)

            def rstd_of(s):
                act.wait_ge(mv_ready, s * 4 + 4)
                nc.scalar.activation(lnv[:], mv[:, :, 1], ACT.Ln, bias=per["eps"][:, 0:1]).then_inc(lnv_ready, 1)
                act.wait_ge(lnv_ready, s + 1)
                nc.scalar.activation(rstd[:], lnv[:], ACT.Exp, scale=-0.5).then_inc(rstd_ready, 1)

            def normalise(s, h):
                act.wait_ge(nmr_ready, s + 1)
                for t in range(TT_):
                    nc.scalar.activation(xin[:, h, t], xin[:, h, t], ACT.Identity, bias=nmr[:, t:t + 1],
                                         scale=rstd[:, t:t + 1]).then_inc(xn_ready, 1)

            def modulate(s, b, cs, first_step):
                act.wait_ge(mod_ready, b + 1)
                act.wait_ge(shift_ready, s + 1)
                if not first_step:
                    act.wait_ge(mixsum_ready, s * 12)
                for c in cs:
                    act.wait_ge(xnT_in_psum, s * 4 + c + 1)
                    nc.scalar.activation(hT[:, c, 1:ST + 1], misc[:, c % 2], ACT.Identity,
                                         bias=mod[:, SHIFT1, c:c + 1], scale=mod[:, SCALE1, c:c + 1]
                                         ).then_inc(hT_ready, 1)

            def mixprods(s, m, cs, old):
                if m == 0 and old:
                    act.wait_ge(mixlo_ready, s * 2 * SPLIT - 2)
                if m == 1 and old:
                    act.wait_ge(in_psum[2], s * 2)
                if m == 2:
                    act.wait_ge(mixlo_ready, s * 2 * SPLIT + 4)
                for c in cs:
                    if m == 0:
                        act.wait_ge(hT_ready, s * 4 + c + 1)
                    nc.scalar.activation(mix[m][:, c], hT[:, c, 1:ST + 1], ACT.Copy,
                                         scale=per["chan"][:, m, c:c + 1]).then_inc(mixprod_ready, 1)

            def mix_leading(s, m, old):
                if old:
                    act.wait_ge(in_psum[m], s * 2)
                for k in range(0, CT, 2):
                    act.wait_ge(mixsum_ready, s * 12 + 4 * m + k + 2)
                    nc.scalar.activation(mix_hi[:, m, k:k + 2], mix[m][:, k:k + 2], ACT.Copy).then_inc(mixhi_ready, 1)

            def evacuate_kv(u, q, m, old):
                act.wait_ge(in_psum[m], u + 1)
                if old and m == 0:
                    act.wait_ge(kp_ready, u)
                if old and m == 1:
                    act.wait_ge(y_ready, u - 1)
                nc.scalar.activation(kb if m == 0 else vb[:, q], proj[m][:], ACT.Copy
                                     ).then_inc(k_ready if m == 0 else v_ready, 1)

            def evacuate_r(u, old):
                act.wait_ge(in_psum[2], u + 1)
                if old:
                    act.wait_ge(logm_ready, u)
                nc.scalar.activation(mb, proj[2][:], ACT.Relu, scale=-1.0).then_inc(m_ready, 1)
                nc.scalar.activation(eb, proj[2][:], ACT.Abs).then_inc(absr_ready, 1)
                act.wait_ge(absr_ready, u + 1)
                nc.scalar.activation(eb, eb, ACT.Exp, scale=-1.0).then_inc(eb_ready, 1)

            def state_weights(u, p):
                act.wait_ge(kp_ready, u + 1)
                for i in range(2):
                    c = 2 * p + i
                    nc.scalar.activation(e1[:, i], kp[:, i], ACT.Relu, bias=per["neg_w"][:, c:c + 1]
                                         ).then_inc(e1_arg, 1)
                    nc.scalar.activation(ha[:, i], kp[:, i], ACT.Relu, bias=per["w"][:, c:c + 1], scale=-1.0
                                         ).then_inc(ha_arg, 1)
                act.wait_ge(e1_arg, u * 2 + 2)
                nc.scalar.activation(e1[:], e1[:], ACT.Exp, scale=-1.0).then_inc(e1_ready, 1)
                act.wait_ge(ha_arg, u * 2 + 2)
                nc.scalar.activation(ha[:], ha[:], ACT.Exp, scale=-1.0).then_inc(ha_ready, 1)

            def output_weights(u, p, old):
                if old:
                    act.wait_ge(y_ready, u)
                for i in range(2):
                    c = 2 * p + i
                    nc.scalar.activation(ga[:, i], kp[:, i], ACT.Relu, bias=per["neg_u"][:, c:c + 1], scale=-1.0
                                         ).then_inc(ga_arg, 1)
                    nc.scalar.activation(gb[:, i], kp[:, i], ACT.Relu, bias=per["chan"][:, 4, c:c + 1]
                                         ).then_inc(gb_arg, 1)
                act.wait_ge(ga_arg, u * 2 + 2)
                nc.scalar.activation(ga[:], ga[:], ACT.Exp, scale=-1.0).then_inc(ga_ready, 1)
                act.wait_ge(gb_arg, u * 2 + 2)
                nc.scalar.activation(gb[:], gb[:], ACT.Exp, scale=-1.0).then_inc(gb_ready, 1)

            def log_den(u):
                act.wait_ge(full_den_ready, u + 1)
                nc.scalar.activation(ga[:], ga[:], ACT.Ln).then_inc(log_ready, 1)

            def inverse(u):
                act.wait_ge(logm_ready, u + 1)
                nc.scalar.activation(ga[:], ga[:], ACT.Exp, scale=-1.0).then_inc(inv_ready, 1)

            act.add_instruction(mybir.InstLoadActFuncSet(name=nc.get_next_instruction_name(),
                                                         act_func_set_id=LN_EXP_SET, ins=[], outs=[]))
            act.wait_ge(cT_in_psum, 1)
            nc.scalar.activation(silu_exp[:], cT_ps, ACT.Exp, scale=-1.0).then_inc(c_exp_ready, 1)
            act.wait_ge(chan_ready, 1)
            nc.scalar.activation(per["neg_w"][:], per["chan"][:, 3, :], ACT.Exp).then_inc(decay_ready, 1)
            act.wait_ge(eps_ready, 1)
            transposed_weights(0)
            transposed_weights(1)
            rstd_of(0)
            normalise(0, 0)
            act.wait_ge(mod_rows_in_psum, 1)
            nc.scalar.activation(mod_rows[:, 0], proj[1][0:B, 0], ACT.Copy).then_inc(mod_rows_ready, 1)
            modulate(0, 0, range(CT), True)
            mixprods(0, 0, range(CT), False)
            transposed_weights(2)
            mix_leading(0, 0, False)
            mixprods(0, 1, range(CT), False)
            transposed_weights(3)
            mix_leading(0, 1, False)
            mixprods(0, 2, range(CT), False)
            rstd_of(1)
            evacuate_kv(0, 0, 0, False)
            normalise(1, 1)
            state_weights(0, 0)
            evacuate_kv(0, 0, 1, False)
            output_weights(0, 0, False)

            def batch(b, first, last):
                for h in range(2):
                    s = b * 2 + h
                    u = b * 4 + 2 * h
                    ahead = not (last and h == 1)
                    nb = b + h
                    behind = not (first and h == 0)
                    if ahead:
                        modulate(s + 1, nb, range(0, 2), False)
                    evacuate_r(u, behind)
                    if ahead:
                        mixprods(s + 1, 0, range(0, 2), True)
                    log_den(u)
                    evacuate_kv(u + 1, 1, 0, True)
                    if ahead:
                        modulate(s + 1, nb, range(2, 4), False)
                    inverse(u)
                    if ahead:
                        mixprods(s + 1, 0, range(2, 4), True)
                    state_weights(u + 1, 1)
                    if ahead:
                        mix_leading(s + 1, 0, True)
                    evacuate_kv(u + 1, 1, 1, behind)
                    if ahead:
                        mixprods(s + 1, 1, range(CT), True)
                    output_weights(u + 1, 1, True)
                    if ahead:
                        mix_leading(s + 1, 1, True)
                    if not last:
                        rstd_of(s + 2)
                    evacuate_r(u + 1, True)
                    if ahead:
                        evacuate_kv(u + 2, 0, 0, True)
                        mixprods(s + 1, 2, range(CT), True)
                    log_den(u + 1)
                    if not last:
                        normalise(s + 2, h)
                    inverse(u + 1)
                    if ahead:
                        state_weights(u + 2, 0)
                        evacuate_kv(u + 2, 0, 1, True)
                        output_weights(u + 2, 0, True)
            over_batches(act, batch)
            for q in range(2):
                act.wait_ge(mod2_rows_in_psum, q + 1)
                nc.scalar.activation(mod2_rows[:, q], proj[0][0:B, q], ACT.Copy).then_inc(mod2_rows_ready, 1)

        @block.tensor
        def _(pe):
            def transposes(s, h, cs, old):
                pe.wait_ge(xn_ready, s * 4 + 4)
                for c in cs:
                    if c >= 2:
                        pe.wait_ge(hT_ready, s * 4 + c - 1)
                    elif old:
                        pe.wait_ge(res_ready, s * 4 - 9 + c)
                    for t in range(TT_):
                        last = nc.tensor.transpose(misc[:, c % 2, t * P:(t + 1) * P], xin[:, h, t, c * P:(c + 1) * P],
                                                   per["ident"][:])
                    last.then_inc(xnT_in_psum, 1)

            def project(s, h, p, u, ms, old):
                for m in ms:
                    if m < SPLIT:
                        pe.wait_ge(mixlo_ready, s * 2 * SPLIT + 2 * m + 2)
                    else:
                        pe.wait_ge(mixsum_ready, s * 12 + 4 * m + 4)
                    if old:
                        pe.wait_ge((k_ready, v_ready, absr_ready)[m], u)
                    for i in range(2):
                        d = 2 * p + i
                        for c in range(CT):
                            if m < SPLIT:
                                hi, lo = (per[w][:, m, c, d * P:(d + 1) * P] for w in ("wT_hi", "wT_lo"))
                                nc.tensor.matmul(proj[m][:, i], hi, mix_hi[:, m, c], start=(c == 0), stop=False)
                                nc.tensor.matmul(proj[m][:, i], hi, mix_lo[:, m, c], start=False, stop=False)
                                last = nc.tensor.matmul(proj[m][:, i], lo, mix_hi[:, m, c], start=False,
                                                        stop=(c == CT - 1))
                            else:
                                last = nc.tensor.matmul(proj[m][:, i], per["wT"][:, m - SPLIT, c, d * P:(d + 1) * P],
                                                        mix[m][:, c], start=(c == 0), stop=(c == CT - 1))
                    last.then_inc(in_psum[m], 1)

            def out_project(s, b, h, ts, ahead):
                pe.wait_ge(wo_ready, b * 4 + 4)
                pe.wait_ge(y_ready, s * 2 + 2)
                for t in ts:
                    if t >= 2:
                        pe.wait_ge(res_ready, s * 4 + t - 1)
                    elif ahead:
                        pe.wait_ge(hT_ready, s * 4 + 8 + t + 3)
                    else:
                        pe.wait_ge(res_ready, s * 4 - 1 + t)
                    for c in range(CT):
                        last = nc.tensor.matmul(misc[:, t % 2], yT[:, h, c, t * P:(t + 1) * P], wo_ga[:, c],
                                                start=(c == 0), stop=(c == CT - 1))
                    last.then_inc(o_in_psum, 1)

            def transpose_weights(m):
                pe.wait_ge(w_loaded[m], 16)
                for c in range(CT):
                    before = 4 * m + c - 2
                    if before >= 4 * SPLIT:
                        pe.wait_ge((wt_even, wt_odd)[c % 2], (before - 4 * SPLIT) // 2 + 1)
                    elif before >= 0:
                        pe.wait_ge(wt_lo_ready, before + 1)
                    for t in range(CT):
                        last = nc.tensor.transpose(proj[2][:, c % 2, t * P:(t + 1) * P],
                                                   w_raw[m][:, t, c * P:(c + 1) * P], per["ident"][:])
                    last.then_inc(wt_in_psum, 1)

            def modulation(dest, w, col):
                for k in range(CT):
                    last = nc.tensor.matmul(dest, siluT[:, k, :], w[:, k, col * C:(col + 1) * C], start=(k == 0),
                                            stop=(k == CT - 1))
                return last

            def gates():
                pe.wait_ge(hT_ready, 8)
                pe.wait_ge(wmod_ga_loaded, 16)
                modulation(misc[0:B, 0], wmod_ga, 0)
                pe.wait_ge(wmod_gb_loaded, 16)
                modulation(misc[0:B, 1], wmod_gb, 0).then_inc(gates_in_psum, 1)

            pe.wait_ge(ident_ready, 1)
            pe.wait_ge(chan_loaded, 80)
            nc.tensor.transpose(chan_ps, chan_rows, per["ident"][0:5 * CT, 0:5 * CT]).then_inc(chan_in_psum, 1)
            pe.wait_ge(c_loaded, 16)
            for k in range(CT):
                last = nc.tensor.transpose(cT_ps[:, k, :], c_in[:, k * P:(k + 1) * P], per["ident"][0:B, 0:B])
            last.then_inc(cT_in_psum, 1)
            transpose_weights(MK)
            transpose_weights(MV)
            pe.wait_ge(silu_step, 3)
            pe.wait_ge(wmod1_loaded, 16)
            modulation(proj[1][0:B, SCALE1], wmod1, 1).then_inc(mod_rows_in_psum, 1)
            modulation(proj[1][0:B, SHIFT1], wmod1, 0).then_inc(mod_rows_in_psum, 1)
            pe.wait_ge(chan_ready, 1)
            transposes(0, 0, range(0, 2), False)
            pe.wait_ge(mod_rows_ready, 2)
            for q in range(2):
                for c in range(CT):
                    last = nc.tensor.transpose(mod1_ps[:, q, c, :], mod_rows[:, q, c * P:(c + 1) * P],
                                               per["ident"][0:B, 0:B])
            last.then_inc(mod1_in_psum, 1)
            transposes(0, 0, range(2, CT), False)
            transpose_weights(MR)
            transpose_weights(MO)
            pe.wait_ge(wt_lo_ready, 8)
            project(0, 0, 0, 0, range(0, 1), False)
            pe.wait_ge(mod1_ready, 2)
            project(0, 0, 0, 0, range(1, 2), False)
            pe.wait_ge(wt_even, 4)
            pe.wait_ge(wt_odd, 4)
            project(0, 0, 0, 0, range(2, 3), False)

            def batch(b, first, last):
                for h in range(2):
                    s = b * 2 + h
                    u = b * 4 + 2 * h
                    ahead = not (last and h == 1)
                    if ahead:
                        if first:
                            pe.wait_ge(hT_ready, s * 4 + 4)
                        if first and h == 1:
                            pe.wait_ge(gates_taken, 3)
                        transposes(s + 1, 1 - h, range(0, 2), not first)
                    project(s, h, 1, u + 1, range(0, 1), True)
                    if ahead:
                        transposes(s + 1, 1 - h, range(2, 4), not first)
                    project(s, h, 1, u + 1, range(1, 3), True)
                    behind = not (first and h == 0)
                    if behind:
                        out_project(s - 1, b - 1 + h, 1 - h, range(0, 2), ahead)
                    else:
                        gates()
                    if ahead:
                        project(s + 1, 1 - h, 0, u + 2, range(0, 1), True)
                    if behind:
                        out_project(s - 1, b - 1 + h, 1 - h, range(2, 4), ahead)
                    if ahead:
                        project(s + 1, 1 - h, 0, u + 2, range(1, 3), True)
            over_batches(pe, batch)
            pe.wait_ge(wmod2_loaded, 16)
            pe.wait_ge(k_ready, STEPS * 2)
            for q in range(2):
                for k in range(CT):
                    last = nc.tensor.matmul(proj[0][0:B, q], siluT[:, k, :], wmod2[:, k, 1 - q], start=(k == 0),
                                            stop=(k == CT - 1))
                last.then_inc(mod2_rows_in_psum, 1)
            pe.wait_ge(v_ready, STEPS * 2)
            pe.wait_ge(mod2_rows_ready, 2)
            for q in range(2):
                for c in range(CT):
                    last = nc.tensor.transpose(mod2_ps[:, q, c, :], mod2_rows[:, q, c * P:(c + 1) * P],
                                               per["ident"][0:B, 0:B])
            last.then_inc(mod2_in_psum, 1)
            out_project(STEPS - 1, B - 1, 1, range(TT_), False)

        @block.vector
        def _(dve):
            def stats(s, h, x_count, ts, old):
                if old:
                    dve.wait_ge(lnv_ready, s)
                dve.wait_ge(x_loaded[h], x_count)
                for t in ts:
                    nc.vector.bn_stats(bn6[:, t], xin[:, h, t]).then_inc(bn_ready, 1)

            def aggregate():
                for t in range(TT_):
                    nc.vector.bn_aggr(mv[:, t], bn6[:, t]).then_inc(mv_ready, 1)

            def neg_mean_rstd(s, old):
                if old:
                    dve.wait_ge(xn_ready, s * 4)
                dve.wait_ge(mv_ready, s * 4 + 4)
                dve.wait_ge(rstd_ready, s + 1)
                nc.vector.scalar_tensor_tensor(out=nmr[:], in0=mv[:, :, 0], scalar=-1.0, in1=rstd[:],
                                               op0=ALU.mult, op1=ALU.mult).then_inc(nmr_ready, 1)

            def shift(s, h, first_step):
                if not first_step:
                    dve.wait_ge(mixsum_ready, s * 12)
                if h == 0:
                    nc.vector.memset(hT[:, :, 0], 0.0).then_inc(shift_ready, 1)
                else:
                    dve.wait_ge(hT_ready, s * 4)
                    nc.vector.tensor_copy(hT[:, :, 0], hT[:, :, ST]).then_inc(shift_ready, 1)

            def batch_mod(b, wait_free):
                if wait_free:
                    dve.wait_ge(hT_ready, b * 8)
                nc.vector.tensor_copy(mod[:], per["modT"][:, bass.ds(b, 1), 0:2, :].rearrange("p o q c -> p (o q) c")
                                      ).then_inc(mod_ready, 1)

            def add_shifted(s, m, cs):
                for c in cs:
                    if m == 0 and c == 0:
                        dve.wait_ge(shift_ready, s + 1)
                    dve.wait_ge(mixprod_ready, s * 12 + 4 * m + c + 1)
                    nc.vector.scalar_tensor_tensor(out=mix[m][:, c], in0=hT[:, c, 0:ST],
                                                   scalar=per["one_less_mix"][:, m, c:c + 1], in1=mix[m][:, c],
                                                   op0=ALU.mult, op1=ALU.add).then_inc(mixsum_ready, 1)

            def mix_rest(s, m, ks):
                for k in ks:
                    dve.wait_ge(mixhi_ready, s * 2 * SPLIT + 2 * m + k // 2 + 1)
                    nc.vector.tensor_tensor(mix_lo[:, m, k:k + 2], mix[m][:, k:k + 2], mix_hi[:, m, k:k + 2],
                                            ALU.subtract).then_inc(mixlo_ready, 1)

            def state_start(u, p, h):
                st = state[:, p]
                if h == 0:
                    nc.vector.memset(st[:, 0, :, 0], NEG_HUGE).then_inc(init_ready, 1)
                    nc.vector.memset(st[:, 1:3, :, 0], 0.0).then_inc(init_ready, 1)
                else:
                    nc.vector.tensor_copy(st[:, 0, :, 0], st[:, 0, :, ST]).then_inc(init_ready, 1)
                    nc.vector.tensor_copy(st[:, 1:3, :, 0], st[:, 1:3, :, ST]).then_inc(init_ready, 1)

            def running_max(u, p):
                st = state[:, p]
                dve.wait_ge(k_ready, u + 1)
                dve.wait_ge(init_ready, u * 2 + 2)
                for i in range(2):
                    c = 2 * p + i
                    nc.vector.tensor_tensor_scan(st[:, 0, i, 1:ST + 1], per["w"][:, c:c + 1].to_broadcast([P, ST]),
                                                 kb[:, i], st[:, 0, i, 0:1], ALU.add, ALU.max
                                                 ).then_inc(max_ready, 1)
                dve.wait_ge(max_ready, u * 2 + 2)
                nc.vector.tensor_tensor(kp[:], kb[:], st[:, 0, :, 0:ST], ALU.subtract).then_inc(kp_ready, 1)

            def denominator_states(u, p):
                st = state[:, p]
                dve.wait_ge(ha_ready, u + 1)
                dve.wait_ge(e1_ready, u + 1)
                for i in range(2):
                    nc.vector.tensor_tensor_scan(st[:, 2, i, 1:ST + 1], e1[:, i], ha[:, i], st[:, 2, i, 0:1],
                                                 ALU.mult, ALU.add).then_inc(den_state, 1)

            def weighted_values(u, q):
                dve.wait_ge(v_ready, u + 1)
                dve.wait_ge(den_state, u * 2 + 2)
                nc.vector.tensor_tensor(ha[:], ha[:], vb[:, q], ALU.mult).then_inc(e2v_ready, 1)

            def numerator_states(u, p):
                st = state[:, p]
                dve.wait_ge(e2v_ready, u + 1)
                for i in range(2):
                    nc.vector.tensor_tensor_scan(st[:, 1, i, 1:ST + 1], e1[:, i], ha[:, i], st[:, 1, i, 0:1],
                                                 ALU.mult, ALU.add).then_inc(num_state, 1)

            def outputs(u, p, q):
                st = state[:, p]
                dve.wait_ge(e2v_ready, u + 1)
                dve.wait_ge(ga_ready, u + 1)
                nc.vector.tensor_tensor(vb[:, q], ga[:], vb[:, q], ALU.mult).then_inc(n2_ready, 1)
                dve.wait_ge(gb_ready, u + 1)
                dve.wait_ge(num_state, u * 2 + 2)
                state_part = gb.rearrange("p (o i) t -> p o i t", o=1).to_broadcast([P, 2, 2, ST])
                nc.vector.tensor_tensor(state_bufs[:], state_part, st[:, 1:3, :, 0:ST], ALU.mult
                                        ).then_inc(state_out, 1)

            def denominator(u):
                dve.wait_ge(state_out, u + 1)
                nc.vector.tensor_tensor(ga[:], ga[:], ha[:], ALU.add).then_inc(den_ready, 1)

            def full_denominator(u, q):
                dve.wait_ge(eb_ready, u + 1)
                dve.wait_ge(den_ready, u + 1)
                nc.vector.scalar_tensor_tensor(out=ga[:], in0=eb, scalar=1.0, in1=ga[:], op0=ALU.add,
                                               op1=ALU.mult).then_inc(full_den_ready, 1)
                dve.wait_ge(n2_ready, u + 1)
                nc.vector.tensor_tensor(vb[:, q], vb[:, q], e1[:], ALU.add).then_inc(num_ready, 1)

            def log_plus_m(u):
                dve.wait_ge(log_ready, u + 1)
                dve.wait_ge(m_ready, u + 1)
                nc.vector.tensor_tensor(ga[:], ga[:], mb, ALU.add).then_inc(logm_ready, 1)

            def output(u, p, q, h, s, wait_free):
                if wait_free:
                    dve.wait_ge(o_in_psum, s * 4 - 4)
                dve.wait_ge(num_ready, u + 1)
                dve.wait_ge(inv_ready, u + 1)
                nc.vector.tensor_tensor(yT[:, h, 2 * p:2 * p + 2], vb[:, q], ga[:], ALU.mult).then_inc(y_ready, 1)

            def gate_projection(b):
                dve.wait_ge(o_in_psum, b * 8)
                dve.wait_ge(gate_loaded, b * 16 + 16)
                for c in range(CT):
                    nc.vector.tensor_tensor(wo_ga[:, c], per["wT"][:, MO - SPLIT, c], gate[:], ALU.mult
                                            ).then_inc(wo_ready, 1)

            def residual(step, ts):
                for t in ts:
                    dve.wait_ge(o_in_psum, step * 4 + t + 1)
                    dve.wait_ge(xres_loaded, step * 16 + 16)
                    nc.vector.tensor_tensor(xres[:, t], misc[:, t % 2], xres[:, t], ALU.add).then_inc(res_ready, 1)

            def transposed_weights(m):
                if m < SPLIT:
                    for c in range(CT):
                        dve.wait_ge(wt_hi_ready, 4 * m + c + 1)
                        nc.vector.tensor_tensor(per["wT_lo"][:, m, c, :], proj[2][:, c % 2], per["wT_hi"][:, m, c, :],
                                                ALU.subtract).then_inc(wt_lo_ready, 1)
                else:
                    for c in range(1, CT, 2):
                        dve.wait_ge(wt_in_psum, 4 * m + c + 1)
                        nc.vector.tensor_copy(per["wT"][:, m - SPLIT, c, :], proj[2][:, 1]).then_inc(wt_odd, 1)

            def modulation_rows(ps, first_row, done):
                for q in range(2):
                    nc.vector.tensor_scalar(per["modT"][:, :, first_row + q, :].rearrange("p b c -> p c b"), ps[:, q],
                                            1.0 - q, None, ALU.add).then_inc(done, 1)

            dve.wait_ge(chan_in_psum, 1)
            nc.vector.tensor_copy(per["chan"][:].rearrange("p i c -> p (i c)"), chan_ps).then_inc(chan_ready, 1)
            dve.wait_ge(c_exp_ready, 1)
            nc.vector.tensor_scalar(silu_den[:], silu_exp[:], 1.0, None, ALU.add).then_inc(silu_step, 1)
            dve.wait_ge(silu_step, 1)
            nc.vector.reciprocal(silu_rec[:], silu_den[:]).then_inc(silu_step, 1)
            dve.wait_ge(silu_step, 2)
            nc.vector.tensor_tensor(siluT[:], cT_ps, silu_rec[:], ALU.mult).then_inc(silu_step, 1)
            dve.wait_ge(chan_ready, 1)
            nc.vector.tensor_scalar(per["one_less_mix"][:], per["chan"][:, 0:3, :], -1.0, 1.0, ALU.mult, ALU.add
                                    ).then_inc(const_ready, 1)
            nc.vector.tensor_scalar(per["neg_u"][:], per["chan"][:, 4, :], -1.0, None, ALU.mult
                                    ).then_inc(const_ready, 1)
            dve.wait_ge(decay_ready, 1)
            nc.vector.tensor_scalar(per["w"][:], per["neg_w"][:], -1.0, None, ALU.mult).then_inc(const_ready, 1)
            transposed_weights(0)
            transposed_weights(1)
            stats(0, 0, 16, range(TT_), False)
            dve.wait_ge(bn_ready, 4)
            shift(0, 0, True)
            aggregate()
            neg_mean_rstd(0, False)
            dve.wait_ge(mod_rows_in_psum, 2)
            nc.vector.tensor_copy(mod_rows[:, 1], proj[1][0:B, 1]).then_inc(mod_rows_ready, 1)
            dve.wait_ge(mod1_in_psum, 1)
            modulation_rows(mod1_ps, SCALE1, mod1_ready)
            dve.wait_ge(mod1_ready, 2)
            batch_mod(0, False)
            dve.wait_ge(const_ready, 3)
            add_shifted(0, 0, range(CT))
            transposed_weights(2)
            mix_rest(0, 0, (0, 2))
            add_shifted(0, 1, range(CT))
            transposed_weights(3)
            mix_rest(0, 1, (0, 2))
            stats(1, 1, 16, range(TT_), True)
            dve.wait_ge(bn_ready, 8)
            add_shifted(0, 2, range(CT))
            aggregate()
            neg_mean_rstd(1, True)
            state_start(0, 0, 0)
            running_max(0, 0)
            def gates():
                dve.wait_ge(gates_in_psum, 1)
                nc.vector.tensor_scalar(gate_rows, misc[0:B], 0.0, 2.0, ALU.is_ge, ALU.mult).then_inc(gates_taken, 1)
                nc.vector.tensor_scalar(gate_abs, misc[0:B], -1.0, None, ALU.mult).then_inc(gates_taken, 1)
                dve.wait_ge(gates_taken, 2)
                nc.vector.scalar_tensor_tensor(out=gate_abs, in0=gate_abs, scalar=GATE_FLOOR, in1=misc[0:B],
                                               op0=ALU.max, op1=ALU.max).then_inc(gates_taken, 1)
                dve.wait_ge(gates_taken, 3)
                nc.vector.scalar_tensor_tensor(out=gate_rows, in0=gate_rows, scalar=1.0, in1=gate_abs,
                                               op0=ALU.subtract, op1=ALU.mult).then_inc(gate_rows_ready, 1)

            def batch(b, first, last):
                for h in range(2):
                    s = b * 2 + h
                    u = b * 4 + 2 * h
                    ahead = not (last and h == 1)
                    behind = not (first and h == 0)
                    if ahead:
                        if h == 1:
                            batch_mod(b + 1, True)
                        shift(s + 1, 1 - h, False)
                    if not last:
                        stats(s + 2, h, b * 16 + 32, range(0, 3), True)
                    denominator_states(u, 0)
                    weighted_values(u, 0)
                    if not last:
                        stats(s + 2, h, b * 16 + 32, range(3, TT_), True)
                    numerator_states(u, 0)
                    outputs(u, 0, 0)
                    state_start(u + 1, 1, h)
                    denominator(u)
                    full_denominator(u, 0)
                    log_plus_m(u)
                    running_max(u + 1, 1)
                    if h == 1:
                        gate_projection(b)
                    if ahead:
                        add_shifted(s + 1, 0, range(0, 2))
                    output(u, 0, 0, h, s, not first)
                    if ahead:
                        add_shifted(s + 1, 0, range(2, 4))
                    if not last:
                        dve.wait_ge(bn_ready, s * 4 + 12)
                    denominator_states(u + 1, 1)
                    if not last:
                        aggregate()
                    if ahead:
                        mix_rest(s + 1, 0, (0,))
                    weighted_values(u + 1, 1)
                    if ahead:
                        mix_rest(s + 1, 0, (2,))
                    numerator_states(u + 1, 1)
                    if ahead:
                        add_shifted(s + 1, 1, range(CT))
                    if behind:
                        residual(s - 1, range(0, 2))
                    if ahead:
                        mix_rest(s + 1, 1, (0, 2))
                    if not last:
                        neg_mean_rstd(s + 2, True)
                    outputs(u + 1, 1, 1)
                    if ahead:
                        state_start(u + 2, 0, 1 - h)
                        add_shifted(s + 1, 2, range(0, 1))
                    denominator(u + 1)
                    if ahead:
                        add_shifted(s + 1, 2, range(1, 2))
                    full_denominator(u + 1, 1)
                    if ahead:
                        add_shifted(s + 1, 2, range(2, 4))
                    log_plus_m(u + 1)
                    if ahead:
                        running_max(u + 2, 0)
                    output(u + 1, 1, 1, h, s, not first)
                    if behind:
                        residual(s - 1, range(2, 4))
                    else:
                        gates()
            over_batches(dve, batch)
            dve.wait_ge(mod2_in_psum, 1)
            modulation_rows(mod2_ps, SCALE2, mod2_ready)
            residual(STEPS - 1, range(TT_))


def ffn(nc, io, per, out):
    with ExitStack() as ctx:
        def sb(name, shape, dt=F32):
            return ctx.enter_context(nc.sbuf_tensor(name, shape, dt))

        def sem(name):
            return ctx.enter_context(nc.semaphore(name))

        xT_hi = sb("xT_hi", [P, CT, NTOK], F32R)
        xT_lo = sb("xT_lo", [P, CT, NTOK], F32R)
        w1_hi = sb("w1_hi", [P, 2, CT, FT * P], F32R)
        w1_lo = sb("w1_lo", [P, 2, CT, FT * P], F32R)
        w2_hi = sb("w2_hi", [P, 2, FT, C], F32R)
        w2_lo = sb("w2_lo", [P, 2, FT, C], F32R)
        wraw = sb("ffn_wraw", [P, CT, C])
        y = sb("y", [P, TOKT, C])
        h_raw = sb("h_raw", [P, 2, ST])
        h_hi = sb("h_hi", [P, 2, FT, ST], F32R)
        h_lo = sb("h_lo", [P, 2, FT, ST], F32R)
        bn6 = sb("ffn_bn6", [P, TOKT, 6])
        mv = sb("ffn_mv", [P, TOKT, 2])
        lnv = sb("ffn_lnv", [P, TOKT])
        rstd = sb("ffn_rstd", [P, TOKT])
        nmr = sb("ffn_nmr", [P, TOKT])
        ew = sb("ew", [P, TOKT, 2])
        wsum = sb("wsum", [P, TOKT])
        gate = wraw[:, 0:2]
        x1 = sb("x1", [P, 2, TT_, C])
        up = ctx.enter_context(nc.psum_tensor("up", [P, FT, ST], F32))
        down = ctx.enter_context(nc.psum_tensor("down", [P, TT_, C], F32))

        x_tile_loaded = [sem(f"ffn_x_tile_loaded{t}") for t in range(TT_)]
        x_loaded = [sem(f"ffn_x_loaded{c}") for c in range(CHUNKS)]
        ew_loaded = sem("ew_loaded")
        gates_loaded = sem("gates_loaded")
        wraw_loaded = [sem("w1_loaded"), sem("w2_loaded")]
        bn_ready = sem("ffn_bn_ready")
        mv_ready = sem("ffn_mv_ready")
        lnv_ready = sem("ffn_lnv_ready")
        rstd_ready = sem("ffn_rstd_ready")
        nmr_ready = sem("ffn_nmr_ready")
        xn_ready = sem("ffn_xn_ready")
        xn_late_ready = sem("ffn_xn_late_ready")
        xnT_in_psum = sem("ffn_xnT_in_psum")
        xT_ready = sem("ffn_xT_ready")
        xhi_ready = sem("xhi_ready")
        xlo_ready = sem("xlo_ready")
        wsum_ready = sem("wsum_ready")
        zero_ready = sem("y_zeroed")
        whi_ready = [sem("w1_hi_ready"), sem("w2_hi_ready")]
        wlo_ready = [sem("w1_lo_ready"), sem("w2_lo_ready")]
        h_in_psum = sem("h_in_psum")
        gelu_ready = sem("gelu_ready")
        hhi_ready = sem("hhi_ready")
        hlo_ready = sem("hlo_ready")
        y_in_psum = sem("y_in_psum")
        y_ready = sem("ffn_y_ready")
        x1_loaded = [sem("x1_loaded0"), sem("x1_loaded1")]
        scaled_ready = sem("scaled_ready")
        sum_ready = sem("sum_ready")
        final_stored = sem("final_stored")

        rows = out[0:NTOK, :].rearrange("(n p) c -> p n c", p=P)
        w_rows = [io["w1"].rearrange("(c p) (g n) -> g p c n", p=P, n=FT * P),
                  io["w2"].rearrange("(g f p) n -> g p f n", f=FT, p=P)]
        w_hi, w_lo = (w1_hi, w2_hi), (w1_lo, w2_lo)
        block = ctx.enter_context(nc.Block())
        JOBS = 2 * CHUNKS
        TURNS = GROUPS // 2

        def over_turns(eng, turn):
            turn(0, True, False)
            with eng.Fori(1, TURNS - 1) as it:
                turn(it, False, False)
            turn(TURNS - 1, False, True)

        @block.sync
        def _(sp):
            for t in range(TT_):
                sp.dma_start(y[:, t], rows[:, t]).then_inc(x_tile_loaded[t], 16)
            sp.dma_start(wraw[:], w_rows[0][0]).then_inc(wraw_loaded[0], 16)
            for c in range(1, CHUNKS):
                sp.dma_start(y[:, 4 * c:4 * c + 4], rows[:, 4 * c:4 * c + 4]).then_inc(x_loaded[c], 16)
            sp.wait_ge(wlo_ready[0], 2)
            sp.dma_start(wraw[:], w_rows[1][0]).then_inc(wraw_loaded[1], 16)
            sp.dma_start(ew[:], io["ew"].rearrange("(n p) k -> p n k", p=P)).then_inc(ew_loaded, 16)
            with sp.Fori(1, GROUPS) as g:
                for i in range(2):
                    if i == 0:
                        sp.wait_ge(wlo_ready[1], g * 2)
                    else:
                        sp.wait_ge(wlo_ready[0], g * 2 + 2)
                    sp.dma_start(wraw[:], w_rows[i][bass.ds(g, 1)].rearrange("o p c n -> (o p) c n")
                                 ).then_inc(wraw_loaded[i], 16)
            for c in range(2):
                sp.dma_start(x1[:, c], rows[:, 4 * c:4 * c + 4]).then_inc(x1_loaded[c], 16)
            sp.wait_ge(wlo_ready[1], GROUPS * 2)
            for b in range(2):
                sp.dma_start(gate[:, b], per["gates"][1, b:b + 1, :].to_broadcast([P, C])).then_inc(gates_loaded, 16)
            for n in range(TOKT):
                sp.wait_ge(sum_ready, n + 1)
                sp.dma_start(rows[:, n], y[:, n]).then_inc(final_stored, 16)
                if n == 3 or n == 7:
                    c = n // 4 + 2
                    sp.dma_start(x1[:, c % 2], rows[:, 4 * c:4 * c + 4]).then_inc(x1_loaded[c % 2], 16)
            sp.wait_ge(final_stored, TOKT * 16)

        @block.scalar
        def _(act):
            def split_weights(g, q, i):
                act.wait_ge(wraw_loaded[i], g * 16 + 16)
                for k in range(2):
                    nc.scalar.activation(w_hi[i][:, q, 2 * k:2 * k + 2], wraw[:, 2 * k:2 * k + 2], ACT.Copy
                                         ).then_inc(whi_ready[i], 1)

            def gelu(job, q, raw_used, half_used):
                for f in range(FT):
                    act.wait_ge(h_in_psum, job * 4 + f + 1)
                    if raw_used or f >= 2:
                        act.wait_ge(hlo_ready, job * 4 - 1 + f)
                    nc.scalar.activation(h_raw[:, f % 2], up[:, f], ACT.Gelu_apprx_tanh).then_inc(gelu_ready, 1)
                    act.wait_ge(gelu_ready, job * 4 + f + 1)
                    if f == 0 and half_used:
                        act.wait_ge(y_in_psum, job * 4 - 4)
                    nc.scalar.activation(h_hi[:, q, f], h_raw[:, f % 2], ACT.Copy).then_inc(hhi_ready, 1)

            def chunk_rstd(c):
                ts = slice(4 * c, 4 * c + 4)
                act.wait_ge(mv_ready, 4 * c + 4)
                nc.scalar.activation(lnv[:, ts], mv[:, ts, 1], ACT.Ln, bias=per["eps"][:, 0:1]).then_inc(lnv_ready, 1)
                act.wait_ge(lnv_ready, c + 1)
                nc.scalar.activation(rstd[:, ts], lnv[:, ts], ACT.Exp, scale=-0.5).then_inc(rstd_ready, 1)

            def chunk_normalise(c):
                act.wait_ge(nmr_ready, c + 1)
                for t in range(4 * c, 4 * c + 4):
                    nc.scalar.activation(y[:, t], y[:, t], ACT.Identity, bias=nmr[:, t:t + 1], scale=rstd[:, t:t + 1]
                                         ).then_inc(xn_ready, 1)

            def chunk_modulate(c):
                for k in range(CT):
                    act.wait_ge(xnT_in_psum, 4 * c + k + 1)
                    if c == 2 and k < 2:
                        act.wait_ge(hlo_ready, 4)
                    elif 4 * c + k >= 2:
                        act.wait_ge(xlo_ready, 4 * c + k - 1)
                    b = c // 2
                    nc.scalar.activation(h_raw[:, k % 2], down[:, k], ACT.Identity,
                                         bias=per["modT"][:, b, SHIFT2, k:k + 1],
                                         scale=per["modT"][:, b, SCALE2, k:k + 1]).then_inc(xT_ready, 1)
                    act.wait_ge(xT_ready, 4 * c + k + 1)
                    nc.scalar.activation(xT_hi[:, k, c * ST:(c + 1) * ST], h_raw[:, k % 2], ACT.Copy
                                         ).then_inc(xhi_ready, 1)

            chunk_rstd(0)
            chunk_normalise(0)
            split_weights(0, 0, 0)
            chunk_modulate(0)
            chunk_rstd(1)
            chunk_normalise(1)
            chunk_rstd(2)
            chunk_modulate(1)
            chunk_rstd(3)
            act.wait_ge(xlo_ready, 8)
            gelu(0, 0, False, False)
            chunk_modulate(2)
            split_weights(0, 0, 1)
            chunk_modulate(3)
            act.wait_ge(xlo_ready, 4 * CHUNKS)

            def turn(it, first, last):
                for j in range(JOBS):
                    job = it * JOBS + j
                    if not (last and j == JOBS - 1):
                        gelu(job + 1, (j + 1) % 2, True, not (first and j == 0))
                    if j % CHUNKS in (1, 2) and not (last and j > CHUNKS):
                        g = it * 2 + j // CHUNKS
                        if j % CHUNKS == 1 and not (first and j == 1):
                            act.wait_ge(y_in_psum, g * 16)
                        split_weights(g + 1, (j // CHUNKS + 1) % 2, j % CHUNKS - 1)
            over_turns(act, turn)

        @block.gpsimd
        def _(pool):
            for c in range(CHUNKS):
                pool.wait_ge(xnT_in_psum, 4 * c + 4)
                pool.memset(y[:, 4 * c:4 * c + 4], 0.0).then_inc(zero_ready, 1)

        @block.tensor
        def _(pe):
            def first_product(job, g, q, chunk, fs, prologue, group0):
                pe.wait_ge(wlo_ready[0], g * 2 + 2)
                for f in fs:
                    if not prologue:
                        pe.wait_ge(gelu_ready, job * 4 - 3 + f)
                    ft, ts = slice(f * P, (f + 1) * P), slice(chunk * ST, (chunk + 1) * ST)
                    for c in range(CT):
                        if group0 and f == fs[0]:
                            pe.wait_ge(xlo_ready, 4 * chunk + c + 1)
                        hi, lo = w1_hi[:, q, c, ft], w1_lo[:, q, c, ft]
                        nc.tensor.matmul(up[:, f], hi, xT_hi[:, c, ts], start=(c == 0), stop=False)
                        nc.tensor.matmul(up[:, f], hi, xT_lo[:, c, ts], start=False, stop=False)
                        last = nc.tensor.matmul(up[:, f], lo, xT_hi[:, c, ts], start=False, stop=(c == CT - 1))
                    last.then_inc(h_in_psum, 1)

            def second_product(job, g, q, hq, old):
                pe.wait_ge(hlo_ready, job * 4 + 4)
                pe.wait_ge(wlo_ready[1], g * 2 + 2)
                for t in range(TT_):
                    if old:
                        pe.wait_ge(y_ready, job * 4 - 3 + t)
                    else:
                        pe.wait_ge(xT_ready, 4 * CHUNKS)
                    ts = slice(t * P, (t + 1) * P)
                    for f in range(FT):
                        hi, lo = h_hi[:, hq, f, ts], h_lo[:, hq, f, ts]
                        nc.tensor.matmul(down[:, t], hi, w2_hi[:, q, f], start=(f == 0), stop=False)
                        nc.tensor.matmul(down[:, t], hi, w2_lo[:, q, f], start=False, stop=False)
                        last = nc.tensor.matmul(down[:, t], lo, w2_hi[:, q, f], start=False, stop=(f == FT - 1))
                    last.then_inc(y_in_psum, 1)

            def chunk_transposes(c):
                if c < 2:
                    pe.wait_ge(xn_ready, 4 * c + 4)
                else:
                    pe.wait_ge(xn_late_ready, 4 * c - 4)
                for k in range(CT):
                    if c >= 1:
                        pe.wait_ge(xT_ready, 4 * c - 3 + k)
                    for t in range(TT_):
                        last = nc.tensor.transpose(down[:, k, t * P:(t + 1) * P], y[:, 4 * c + t, k * P:(k + 1) * P],
                                                   per["ident"][:])
                    last.then_inc(xnT_in_psum, 1)

            chunk_transposes(0)
            first_product(0, 0, 0, 0, range(0, 2), True, True)
            chunk_transposes(1)
            first_product(0, 0, 0, 0, range(2, 4), True, True)
            first_product(1, 0, 0, 1, range(0, 1), False, True)
            chunk_transposes(2)
            first_product(1, 0, 0, 1, range(1, 3), False, True)
            chunk_transposes(3)
            first_product(1, 0, 0, 1, range(3, 4), False, True)

            def turn(it, first, last):
                for j in range(JOBS):
                    job = it * JOBS + j
                    n = j + 1
                    if not (first and j == 0 or last and j == JOBS - 1):
                        first_product(job + 1, it * 2 + n // CHUNKS, (n // CHUNKS) % 2, n % CHUNKS, range(FT), False,
                                      first and n < CHUNKS)
                    second_product(job, it * 2 + j // CHUNKS, j // CHUNKS, j % 2, not (first and j == 0))
            over_turns(pe, turn)

        @block.vector
        def _(dve):
            def split_rest(g, q, i):
                for k in range(2):
                    dve.wait_ge(whi_ready[i], g * 2 + k + 1)
                    nc.vector.tensor_tensor(w_lo[i][:, q, 2 * k:2 * k + 2], wraw[:, 2 * k:2 * k + 2],
                                            w_hi[i][:, q, 2 * k:2 * k + 2], ALU.subtract
                                            ).then_inc(wlo_ready[i], 1)

            def h_rest(job, q, half_used):
                for f in range(FT):
                    dve.wait_ge(hhi_ready, job * 4 + f + 1)
                    if f == 0 and half_used:
                        dve.wait_ge(y_in_psum, job * 4 - 4)
                    nc.vector.tensor_tensor(h_lo[:, q, f], h_raw[:, f % 2], h_hi[:, q, f], ALU.subtract
                                            ).then_inc(hlo_ready, 1)

            def accumulate(job, chunk, old):
                for t in range(TT_):
                    n = chunk * TT_ + t
                    dve.wait_ge(y_in_psum, job * 4 + t + 1)
                    if old:
                        dve.wait_ge(y_ready, job * 4 - 4 * CHUNKS + t + 1)
                    nc.vector.tensor_tensor(y[:, n], down[:, t], y[:, n], ALU.add).then_inc(y_ready, 1)

            def chunk_stats(c):
                for t in range(4 * c, 4 * c + 4):
                    dve.wait_ge(x_loaded[c] if c else x_tile_loaded[t], 16)
                    nc.vector.bn_stats(bn6[:, t], y[:, t]).then_inc(bn_ready, 1)
                for t in range(4 * c, 4 * c + 4):
                    dve.wait_ge(bn_ready, t + 1)
                    nc.vector.bn_aggr(mv[:, t], bn6[:, t]).then_inc(mv_ready, 1)

            def chunk_neg_mean_rstd(c):
                ts = slice(4 * c, 4 * c + 4)
                dve.wait_ge(mv_ready, 4 * c + 4)
                dve.wait_ge(rstd_ready, c + 1)
                nc.vector.scalar_tensor_tensor(out=nmr[:, ts], in0=mv[:, ts, 0], scalar=-1.0, in1=rstd[:, ts],
                                               op0=ALU.mult, op1=ALU.mult).then_inc(nmr_ready, 1)

            def chunk_normalise(c):
                dve.wait_ge(nmr_ready, c + 1)
                for t in range(4 * c, 4 * c + 4):
                    nc.vector.tensor_scalar(y[:, t], y[:, t], rstd[:, t:t + 1], nmr[:, t:t + 1], ALU.mult, ALU.add
                                            ).then_inc(xn_late_ready, 1)

            def chunk_rest(c):
                for k in range(CT):
                    dve.wait_ge(xhi_ready, 4 * c + k + 1)
                    cs = slice(c * ST, (c + 1) * ST)
                    nc.vector.tensor_tensor(xT_lo[:, k, cs], h_raw[:, k % 2], xT_hi[:, k, cs], ALU.subtract
                                            ).then_inc(xlo_ready, 1)

            chunk_stats(0)
            chunk_neg_mean_rstd(0)
            split_rest(0, 0, 0)
            chunk_rest(0)
            chunk_stats(1)
            chunk_neg_mean_rstd(1)
            chunk_stats(2)
            chunk_neg_mean_rstd(2)
            chunk_stats(3)
            chunk_normalise(2)
            chunk_rest(1)
            chunk_neg_mean_rstd(3)
            chunk_normalise(3)
            h_rest(0, 0, False)
            chunk_rest(2)
            split_rest(0, 0, 1)
            chunk_rest(3)
            dve.wait_ge(ew_loaded, 16)
            nc.vector.tensor_tensor(wsum[:], ew[:, :, 0], ew[:, :, 1], ALU.add).then_inc(wsum_ready, 1)
            dve.wait_ge(zero_ready, CHUNKS)

            def finish(chunk):
                if chunk == 0:
                    dve.wait_ge(gates_loaded, 32)
                    dve.wait_ge(wsum_ready, 1)
                for n in range(4 * chunk, 4 * chunk + 4):
                    dve.wait_ge(y_ready, (GROUPS - 1) * CHUNKS * 4 + n + 1)
                    nc.vector.scalar_tensor_tensor(out=y[:, n], in0=y[:, n], scalar=wsum[:, n:n + 1],
                                                   in1=gate[:, n // (T // P)], op0=ALU.mult, op1=ALU.mult
                                                   ).then_inc(scaled_ready, 1)
                    dve.wait_ge(scaled_ready, n + 1)
                    dve.wait_ge(x1_loaded[chunk % 2], chunk // 2 * 16 + 16)
                    nc.vector.tensor_tensor(y[:, n], y[:, n], x1[:, chunk % 2, n % TT_], ALU.add
                                            ).then_inc(sum_ready, 1)

            def turn(it, first, last):
                for j in range(JOBS):
                    job = it * JOBS + j
                    if not (last and j == JOBS - 1):
                        h_rest(job + 1, (j + 1) % 2, not (first and j == 0))
                    accumulate(job, j % CHUNKS, not (first and j < CHUNKS))
                    if last and j >= CHUNKS:
                        finish(j - CHUNKS)
                    if j % CHUNKS in (1, 2) and not (last and j > CHUNKS):
                        split_rest(it * 2 + j // CHUNKS + 1, (j // CHUNKS + 1) % 2, j % CHUNKS - 1)
            over_turns(dve, turn)


def adaln_rwkv_ffn(nc, io, out):
    with ExitStack() as ctx:
        def sb(name, shape, dt=F32):
            return ctx.enter_context(nc.sbuf_tensor(name, shape, dt))

        scratch = {"gates": nc.dram_tensor("gates", (2, B, C), F32, kind="Internal").ap()}
        per = {
            "ident": sb("ident", [P, P]),
            "eps": sb("eps", [P, 1]),
            "chan": sb("chan", [P, 5, CT]),
            "one_less_mix": sb("one_less_mix", [P, 3, CT]),
            "neg_w": sb("neg_w", [P, CT]),
            "w": sb("w", [P, CT]),
            "neg_u": sb("neg_u", [P, CT]),
            "modT": sb("modT", [P, B, 4, CT]),
            "siluT": sb("siluT", [P, CT, B]),
            "gates": scratch["gates"],
        }
        with ExitStack() as attention_only:
            for name, count, dt in (("wT", 4 - SPLIT, F32), ("wT_hi", SPLIT, F32R), ("wT_lo", SPLIT, F32R)):
                per[name] = attention_only.enter_context(nc.sbuf_tensor(name, [P, count, CT, C], dt))
            attention(nc, io, per, scratch, out)
        ffn(nc, io, per, out)


_INS = {
    "L0_attn_x": "x", "L0_attn_time_decay": "decay", "L0_attn_time_first": "first", "L0_attn_time_mix_k": "mix_k",
    "L0_attn_time_mix_v": "mix_v", "L0_attn_time_mix_r": "mix_r", "L0_attn_Wk": "Wk", "L0_attn_Wv": "Wv",
    "L0_attn_Wr": "Wr", "L0_attn_Wo": "Wo", "L0_ffn_expert_weights": "ew", "L0_ffn_w1": "w1", "L0_ffn_w2": "w2",
    "L0_c": "c", "L0_wmod": "wmod",
}


def kernel(**inputs):
    import numpy as _np
    import concourse.bacc as _bacc
    from concourse import mybir as _mybir
    from concourse.bass_utils import run_bass_kernel_spmd as _run

    nc = _bacc.Bacc("TRN2", target_bir_lowering=False, num_devices=1, dynamic_dma_scratch_size=1024)
    arrays, io = {}, {}
    for name, short in _INS.items():
        a = _np.ascontiguousarray(inputs[name])
        if short == "x":
            a = a.reshape(B * T, C)
        if short.startswith("mix"):
            a = a.reshape(C)
        arrays[f"in_{short}"] = a
        io[short] = nc.dram_tensor(f"in_{short}", a.shape, _mybir.dt.from_np(a.dtype), kind="ExternalInput").ap()
    out = nc.dram_tensor("out_0", (B * T, C), _mybir.dt.float32, kind="ExternalOutput").ap()
    adaln_rwkv_ffn(nc, io, out)
    r = _run(nc, [arrays], core_ids=[0])
    return r.results[0]["out_0"].reshape(B, T, C)
```
